# Optimizing a Trainium2 kernel written in Bass

```python
import numpy as np
import jax
import jax.numpy as jnp

def _softmax(x, axis=-1):
    return jax.nn.softmax(x, axis=axis)

def _gelu(x):
    return jax.nn.gelu(x, approximate=True)

def _silu(x):
    return jax.nn.silu(x)

def _sigmoid(x):
    return jax.nn.sigmoid(x)

def _layernorm(x, axis=-1, eps=1e-05):
    m = jnp.mean(x, axis=axis, keepdims=True)
    v = jnp.var(x, axis=axis, keepdims=True)
    return (x - m) / jnp.sqrt(v + eps)

def _scatter_add(tgt, idx, src, axis=0):
    return tgt.at[idx].add(src)

def _segment_sum(src, seg, n):
    return jax.ops.segment_sum(src, seg, n)
kernel_name = 'mk_prb_d2_jaxref_r4_4783ec'

def setup_inputs(seed: int=0):
    np.random.seed(seed)
    _w = jnp.asarray

    def _L0_attn_setup():
        import jax, jax.numpy as jnp
        import numpy as np
        import math
        HIDDEN = 512
        NUM_HEADS = 16
        HEAD_SIZE = HIDDEN // NUM_HEADS
        BATCH = 2
        SEQ = 512
        key = jax.random.key(seed)
        k_x, k_wq, k_bq, k_wo, k_bo = jax.random.split(key, 5)
        scale_in = 1.0 / math.sqrt(HIDDEN)
        return {'x': jax.random.normal(k_x, (BATCH, SEQ, HIDDEN), dtype=jnp.float32), 'Wqkv': jax.random.normal(k_wq, (HIDDEN, 3 * HIDDEN), dtype=jnp.float32) * scale_in, 'bqkv': jax.random.normal(k_bq, (3 * HIDDEN,), dtype=jnp.float32) * 0.01, 'Wo': jax.random.normal(k_wo, (HIDDEN, HIDDEN), dtype=jnp.float32) * scale_in, 'bo': jax.random.normal(k_bo, (HIDDEN,), dtype=jnp.float32) * 0.01}
    _L0_attn_in = _L0_attn_setup()

    def _L0_ffn_setup():
        import jax, jax.numpy as jnp
        import numpy as np
        B, S, D = (2, 512, 512)
        F = 256
        E = 64
        K = 8
        C = 256
        NORM_TOPK = False

        def _moe(x, gate_w, w_gate, w_up, w_down):
            b, s, d = x.shape
            T = b * s
            x2 = x.reshape(T, d)
            logits = x2 @ gate_w.T
            probs = jax.nn.softmax(logits.astype(jnp.float32), axis=-1)
            top_w, top_i = jax.lax.top_k(probs, K)
            if NORM_TOPK:
                top_w = top_w / jnp.sum(top_w, axis=-1, keepdims=True)
            top_w = top_w.astype(x.dtype)
            flat_e = top_i.reshape(-1)
            flat_w = top_w.reshape(-1)
            tok = jnp.arange(T * K) // K
            onehot = jax.nn.one_hot(flat_e, E, dtype=jnp.int32)
            pos = jnp.sum(jnp.cumsum(onehot, axis=0) * onehot, axis=-1) - 1
            valid = pos < C
            loc = flat_e * C + jnp.minimum(pos, C - 1)
            flat_w = jnp.where(valid, flat_w, 0.0)
            safe_loc = jnp.where(valid, loc, E * C)
            xg = jnp.zeros((E * C + 1, d), dtype=x.dtype).at[safe_loc].set(x2[tok])[:E * C]
            xg = xg.reshape(E, C, d)
            h = jax.nn.silu(jnp.einsum('ecd,edf->ecf', xg, w_gate)) * jnp.einsum('ecd,edf->ecf', xg, w_up)
            y = jnp.einsum('ecf,efd->ecd', h, w_down).reshape(E * C, d)
            y_tok = y[loc] * flat_w[:, None]
            out = jnp.zeros((T, d), dtype=x.dtype).at[tok].add(y_tok)
            return out.reshape(b, s, d)
        key = jax.random.key(seed)
        ks = jax.random.split(key, 5)
        scale = 0.02
        return {'hidden_states': jax.random.normal(ks[0], (B, S, D), dtype=jnp.float32), 'gate_w': jax.random.normal(ks[1], (E, D), dtype=jnp.float32) * scale, 'w_gate': jax.random.normal(ks[2], (E, D, F), dtype=jnp.float32) * scale, 'w_up': jax.random.normal(ks[3], (E, D, F), dtype=jnp.float32) * scale, 'w_down': jax.random.normal(ks[4], (E, F, D), dtype=jnp.float32) * scale}
    _L0_ffn_in = _L0_ffn_setup()

    def _L1_attn_setup():
        import jax, jax.numpy as jnp
        import numpy as np
        D_MODEL, D_STATE, D_CONV, EXPAND = (512, 16, 4, 2)
        D_INNER = EXPAND * D_MODEL
        DT_RANK = -(-D_MODEL // 16)
        B_SZ, L = (2, 256)

        def _mamba_forward(hidden_states, in_proj_w, conv_w, conv_b, x_proj_w, dt_proj_w, dt_proj_b, A, D, out_proj_w):
            proj = jnp.einsum('bld,ed->ble', hidden_states, in_proj_w)
            x, gate = jnp.split(proj, 2, axis=-1)
            xc = x.transpose(0, 2, 1)
            xc = jax.lax.conv_general_dilated(xc, conv_w[:, None, :], window_strides=(1,), padding=[(D_CONV - 1, 0)], feature_group_count=D_INNER, dimension_numbers=('NCH', 'OIH', 'NCH'))
            xc = jax.nn.silu(xc + conv_b[None, :, None])
            xt = xc.transpose(0, 2, 1)
            ssm = jnp.einsum('bld,ed->ble', xt, x_proj_w)
            ts, Bm, Cm = jnp.split(ssm, [DT_RANK, DT_RANK + D_STATE], axis=-1)
            dt = jnp.einsum('blr,dr->bld', ts, dt_proj_w)
            dt = jax.nn.softplus(dt + dt_proj_b)

            def step(state, inp):
                dt_t, x_t, B_t, C_t = inp
                dA = jnp.exp(dt_t[..., None] * A)
                dBx = dt_t[..., None] * B_t[:, None, :] * x_t[..., None]
                state = state * dA + dBx
                y = jnp.einsum('bds,bs->bd', state, C_t)
                return (state, y)
            xs = (dt.transpose(1, 0, 2), xt.transpose(1, 0, 2), Bm.transpose(1, 0, 2), Cm.transpose(1, 0, 2))
            state0 = jnp.zeros((hidden_states.shape[0], D_INNER, D_STATE), jnp.float32)
            _, ys = jax.lax.scan(step, state0, xs)
            y = ys.transpose(1, 0, 2) + xt * D
            y = y * jax.nn.silu(gate)
            return jnp.einsum('bld,ed->ble', y, out_proj_w)
        key = jax.random.key(seed)
        ks = jax.random.split(key, 10)
        s = 0.02
        return {'hidden_states': jax.random.normal(ks[0], (B_SZ, L, D_MODEL), jnp.float32), 'in_proj_w': jax.random.normal(ks[1], (2 * D_INNER, D_MODEL), jnp.float32) * s, 'conv_w': jax.random.normal(ks[2], (D_INNER, D_CONV), jnp.float32) * 0.1, 'conv_b': jax.random.normal(ks[3], (D_INNER,), jnp.float32) * 0.1, 'x_proj_w': jax.random.normal(ks[4], (DT_RANK + 2 * D_STATE, D_INNER), jnp.float32) * s, 'dt_proj_w': jax.random.normal(ks[5], (D_INNER, DT_RANK), jnp.float32) * s, 'dt_proj_b': jax.random.normal(ks[6], (D_INNER,), jnp.float32) * 0.1 - 4.0, 'A': -jax.random.uniform(ks[7], (D_INNER, D_STATE), jnp.float32, 1.0, 16.0), 'D': jnp.ones((D_INNER,), jnp.float32), 'out_proj_w': jax.random.normal(ks[8], (D_MODEL, D_INNER), jnp.float32) * s}
    _L1_attn_in = _L1_attn_setup()

    def _L1_ffn_setup():
        import jax, jax.numpy as jnp
        import numpy as np
        D_MODEL = 512
        D_EXPERT = 2048
        EPS = 1e-08

        def ternary_quant(w):
            scale = jnp.mean(jnp.abs(w)) + EPS
            q = jnp.clip(jnp.round(w / scale), -1.0, 1.0) * scale
            return w + jax.lax.stop_gradient(q - w)
        key = jax.random.key(seed)
        k_x, k_up, k_gate, k_down = jax.random.split(key, 4)
        std_in = 1.0 / np.sqrt(D_MODEL)
        std_exp = 1.0 / np.sqrt(D_EXPERT)
        return {'x': jax.random.normal(k_x, (4, 512, D_MODEL), dtype=jnp.float32), 'W_up': jax.random.normal(k_up, (D_EXPERT, D_MODEL), dtype=jnp.float32) * std_in, 'W_gate': jax.random.normal(k_gate, (D_EXPERT, D_MODEL), dtype=jnp.float32) * std_in, 'W_down': jax.random.normal(k_down, (D_MODEL, D_EXPERT), dtype=jnp.float32) * std_exp}
    _L1_ffn_in = _L1_ffn_setup()
    _d = {'L0_attn_x': _L0_attn_in['x'], 'L0_attn_Wqkv': _L0_attn_in['Wqkv'], 'L0_attn_bqkv': _L0_attn_in['bqkv'], 'L0_attn_Wo': _L0_attn_in['Wo'], 'L0_attn_bo': _L0_attn_in['bo'], 'L0_ffn_gate_w': _L0_ffn_in['gate_w'], 'L0_ffn_w_gate': _L0_ffn_in['w_gate'], 'L0_ffn_w_up': _L0_ffn_in['w_up'], 'L0_ffn_w_down': _L0_ffn_in['w_down'], 'L1_attn_in_proj_w': _L1_attn_in['in_proj_w'], 'L1_attn_conv_w': _L1_attn_in['conv_w'], 'L1_attn_conv_b': _L1_attn_in['conv_b'], 'L1_attn_x_proj_w': _L1_attn_in['x_proj_w'], 'L1_attn_dt_proj_w': _L1_attn_in['dt_proj_w'], 'L1_attn_dt_proj_b': _L1_attn_in['dt_proj_b'], 'L1_attn_A': _L1_attn_in['A'], 'L1_attn_D': _L1_attn_in['D'], 'L1_attn_out_proj_w': _L1_attn_in['out_proj_w'], 'L1_ffn_W_up': _L1_ffn_in['W_up'], 'L1_ffn_W_gate': _L1_ffn_in['W_gate'], 'L1_ffn_W_down': _L1_ffn_in['W_down']}
    _x0 = _d['L0_attn_x']
    _d['L0_attn_x'] = jax.random.normal(jax.random.fold_in(jax.random.key(seed), 1), (2, 1024, 512), dtype=_x0.dtype)
    del _x0
    return _d

def reference(L0_attn_x, L0_attn_Wqkv, L0_attn_bqkv, L0_attn_Wo, L0_attn_bo, L0_ffn_gate_w, L0_ffn_w_gate, L0_ffn_w_up, L0_ffn_w_down, L1_attn_in_proj_w, L1_attn_conv_w, L1_attn_conv_b, L1_attn_x_proj_w, L1_attn_dt_proj_w, L1_attn_dt_proj_b, L1_attn_A, L1_attn_D, L1_attn_out_proj_w, L1_ffn_W_up, L1_ffn_W_gate, L1_ffn_W_down):

    def _L0_attn_ref(x, Wqkv, bqkv, Wo, bo):
        import jax, jax.numpy as jnp
        import numpy as np
        import math
        HIDDEN = 512
        NUM_HEADS = 16
        HEAD_SIZE = HIDDEN // NUM_HEADS
        BATCH = 2
        SEQ = 512
        b, s, _ = x.shape
        kqv = x @ Wqkv + bqkv
        kqv = kqv.reshape(b, s, 3, NUM_HEADS, HEAD_SIZE)
        q = kqv[:, :, 0]
        k = kqv[:, :, 1]
        v = kqv[:, :, 2]
        scores = jnp.einsum('bsnh,btnh->bnst', k, q) / math.sqrt(HEAD_SIZE)
        ones = jnp.ones_like(scores)
        scores = jnp.triu(scores) + -10000.0 * jnp.tril(ones, k=-1)
        attn = jax.nn.softmax(scores, axis=2)
        out = jnp.einsum('bnkq,bknh->bqnh', attn, v)
        out = out.reshape(b, s, NUM_HEADS * HEAD_SIZE)
        return out @ Wo + bo

    def _L0_ffn_ref(hidden_states, gate_w, w_gate, w_up, w_down):
        import jax, jax.numpy as jnp
        import numpy as np
        B, S, D = (2, 512, 512)
        F = 256
        E = 64
        K = 8
        C = 256
        NORM_TOPK = False

        def _moe(x, gate_w, w_gate, w_up, w_down):
            b, s, d = x.shape
            T = b * s
            x2 = x.reshape(T, d)
            logits = x2 @ gate_w.T
            probs = jax.nn.softmax(logits.astype(jnp.float32), axis=-1)
            top_w, top_i = jax.lax.top_k(probs, K)
            if NORM_TOPK:
                top_w = top_w / jnp.sum(top_w, axis=-1, keepdims=True)
            top_w = top_w.astype(x.dtype)
            flat_e = top_i.reshape(-1)
            flat_w = top_w.reshape(-1)
            tok = jnp.arange(T * K) // K
            onehot = jax.nn.one_hot(flat_e, E, dtype=jnp.int32)
            pos = jnp.sum(jnp.cumsum(onehot, axis=0) * onehot, axis=-1) - 1
            valid = pos < C
            loc = flat_e * C + jnp.minimum(pos, C - 1)
            flat_w = jnp.where(valid, flat_w, 0.0)
            safe_loc = jnp.where(valid, loc, E * C)
            xg = jnp.zeros((E * C + 1, d), dtype=x.dtype).at[safe_loc].set(x2[tok])[:E * C]
            xg = xg.reshape(E, C, d)
            h = jax.nn.silu(jnp.einsum('ecd,edf->ecf', xg, w_gate)) * jnp.einsum('ecd,edf->ecf', xg, w_up)
            y = jnp.einsum('ecf,efd->ecd', h, w_down).reshape(E * C, d)
            y_tok = y[loc] * flat_w[:, None]
            out = jnp.zeros((T, d), dtype=x.dtype).at[tok].add(y_tok)
            return out.reshape(b, s, d)
        return _moe(hidden_states, gate_w, w_gate, w_up, w_down)

    def _L1_attn_ref(hidden_states, in_proj_w, conv_w, conv_b, x_proj_w, dt_proj_w, dt_proj_b, A, D, out_proj_w):
        import jax, jax.numpy as jnp
        import numpy as np
        D_MODEL, D_STATE, D_CONV, EXPAND = (512, 16, 4, 2)
        D_INNER = EXPAND * D_MODEL
        DT_RANK = -(-D_MODEL // 16)
        B_SZ, L = (2, 256)

        def _mamba_forward(hidden_states, in_proj_w, conv_w, conv_b, x_proj_w, dt_proj_w, dt_proj_b, A, D, out_proj_w):
            proj = jnp.einsum('bld,ed->ble', hidden_states, in_proj_w)
            x, gate = jnp.split(proj, 2, axis=-1)
            xc = x.transpose(0, 2, 1)
            xc = jax.lax.conv_general_dilated(xc, conv_w[:, None, :], window_strides=(1,), padding=[(D_CONV - 1, 0)], feature_group_count=D_INNER, dimension_numbers=('NCH', 'OIH', 'NCH'))
            xc = jax.nn.silu(xc + conv_b[None, :, None])
            xt = xc.transpose(0, 2, 1)
            ssm = jnp.einsum('bld,ed->ble', xt, x_proj_w)
            ts, Bm, Cm = jnp.split(ssm, [DT_RANK, DT_RANK + D_STATE], axis=-1)
            dt = jnp.einsum('blr,dr->bld', ts, dt_proj_w)
            dt = jax.nn.softplus(dt + dt_proj_b)

            def step(state, inp):
                dt_t, x_t, B_t, C_t = inp
                dA = jnp.exp(dt_t[..., None] * A)
                dBx = dt_t[..., None] * B_t[:, None, :] * x_t[..., None]
                state = state * dA + dBx
                y = jnp.einsum('bds,bs->bd', state, C_t)
                return (state, y)
            xs = (dt.transpose(1, 0, 2), xt.transpose(1, 0, 2), Bm.transpose(1, 0, 2), Cm.transpose(1, 0, 2))
            state0 = jnp.zeros((hidden_states.shape[0], D_INNER, D_STATE), jnp.float32)
            _, ys = jax.lax.scan(step, state0, xs)
            y = ys.transpose(1, 0, 2) + xt * D
            y = y * jax.nn.silu(gate)
            return jnp.einsum('bld,ed->ble', y, out_proj_w)
        return _mamba_forward(hidden_states, in_proj_w, conv_w, conv_b, x_proj_w, dt_proj_w, dt_proj_b, A, D, out_proj_w)

    def _L1_ffn_ref(x, W_up, W_gate, W_down):
        import jax, jax.numpy as jnp
        import numpy as np
        D_MODEL = 512
        D_EXPERT = 2048
        EPS = 1e-08

        def ternary_quant(w):
            scale = jnp.mean(jnp.abs(w)) + EPS
            q = jnp.clip(jnp.round(w / scale), -1.0, 1.0) * scale
            return w + jax.lax.stop_gradient(q - w)
        wu = ternary_quant(W_up)
        wg = ternary_quant(W_gate)
        wd = ternary_quant(W_down)
        up = jnp.einsum('bsd,ed->bse', x, wu)
        gate = jnp.einsum('bsd,ed->bse', x, wg)
        hidden = jax.nn.silu(up) * gate
        return jnp.einsum('bse,de->bsd', hidden, wd)
    x = L0_attn_x
    xn = _layernorm(x, axis=-1)
    x = x + _L0_attn_ref(xn, L0_attn_Wqkv, L0_attn_bqkv, L0_attn_Wo, L0_attn_bo) + _L0_ffn_ref(xn, L0_ffn_gate_w, L0_ffn_w_gate, L0_ffn_w_up, L0_ffn_w_down)
    xn = _layernorm(x, axis=-1)
    x = x + _L1_attn_ref(xn, L1_attn_in_proj_w, L1_attn_conv_w, L1_attn_conv_b, L1_attn_x_proj_w, L1_attn_dt_proj_w, L1_attn_dt_proj_b, L1_attn_A, L1_attn_D, L1_attn_out_proj_w) + _L1_ffn_ref(xn, L1_ffn_W_up, L1_ffn_W_gate, L1_ffn_W_down)
    return x

_drawn_inputs = setup_inputs


def setup_inputs(seed=0):
    import zlib

    import numpy as np

    out = dict(_drawn_inputs(seed))
    spreads = {'L1_attn_D': (1.0, 0.6)}
    factors = {'L0_attn_bqkv': 15.729,
     'L0_attn_bo': 19.04,
     'L0_ffn_gate_w': 8.0,
     'L0_ffn_w_gate': 8.0,
     'L0_ffn_w_up': 8.0,
     'L0_ffn_w_down': 8.0,
     'L1_attn_in_proj_w': 4.52,
     'L1_attn_conv_w': 5.518,
     'L1_attn_conv_b': 5.732,
     'L1_attn_x_proj_w': 8.0,
     'L1_attn_dt_proj_w': 8.0,
     'L1_attn_dt_proj_b': 8.0,
     'L1_attn_A': 8.0,
     'L1_attn_out_proj_w': 3.896,
     'L0_attn_Wqkv': 2.76,
     'L1_ffn_W_up': 8.0,
     'L1_ffn_W_gate': 8.0,
     'L1_ffn_W_down': 8.0}
    for name, (base, spread) in spreads.items():
        noise = np.random.default_rng([zlib.crc32(name.encode()), seed]).standard_normal(out[name].shape)
        drawn = base * np.exp(spread * noise) if base else spread * noise
        out[name] = jnp.asarray(drawn.astype(out[name].dtype))
    for name, factor in factors.items():
        out[name] = (out[name] * factor).astype(out[name].dtype)
    return out
```

```python
from contextlib import ExitStack, contextmanager
import concourse.bass as bass
from concourse import mybir

P = 128
T, D = 2048, 512
NB, L = 2, 1024
KD = D // P
NT = T // P
CH = 512
NC = T // CH
TPC = CH // P
H, HD = 16, 32
HPG = P // HD
NG = H // HPG
E, F, K, CAP = 64, 256, 8, 256
NS = E * CAP
LN_EPS = 1e-5
TURNS = 4
LOGITS_LAG = 4

F32, F32R, BF16 = mybir.dt.float32, mybir.dt.float32r, mybir.dt.bfloat16
I32, U32 = mybir.dt.int32, mybir.dt.uint32
ALU, ACT = mybir.AluOpType, mybir.ActivationFunctionType
AX_X = mybir.AxisListType.X

HI, LO = 0, 1
PRODUCTS = ((HI, LO), (LO, HI), (HI, HI))

def f32(ap):
    return ap.bitcast(F32)

@contextmanager
def semaphores(nc, tag):
    given = []

    def sem(name):
        given.append(nc.alloc_semaphore(name=f"{tag}_{name}"))
        return given[-1]
    yield sem
    nc.clear_and_free_semaphores(given)
    nc.all_engine_barrier()

def norm_phase(nc, consts, tag, x, xn_rows, xnT, router=None):
    with ExitStack() as ctx:
        sb = lambda name, shape, dt: ctx.enter_context(nc.sbuf_tensor(f"{tag}_{name}", shape, dt))
        ps = lambda name, shape, dt: ctx.enter_context(nc.psum_tensor(f"{tag}_{name}", shape, dt))
        sem = ctx.enter_context(semaphores(nc, tag))

        x_sb = sb("x", [P, NT, D], F32)
        xn = sb("xn", [P, NT, D], F32)
        xT = [sb("xT_hi", [P, NC, KD, CH], F32R), sb("xT_lo", [P, NC, KD, CH], F32R)]
        stats = sb("stats", [P, NT, 6], F32)
        moments = sb("moments", [P, NT, 2], F32)
        std = sb("std", [P, NT], F32)
        rstd = sb("rstd", [P, NT], F32)
        eps = sb("eps", [P, 1], F32)
        ident = sb("ident", [P, P], F32)
        xT_ps = ps("xT_ps", [P, TURNS, KD, P], F32)

        x_loaded, ident_loaded = [sem(f"x_loaded{c}") for c in range(NC)], sem("ident_loaded")
        eps_set, stats_done, moments_done, std_done, rstd_done = (
            sem(n) for n in ("eps_set", "stats_done", "moments_done", "std_done", "rstd_done"))
        xn_done, transposed, hi_done, lo_done = (sem(n) for n in ("xn_done", "transposed", "hi_done", "lo_done"))
        rows_stored, hi_stored, lo_stored = (sem(n) for n in ("rows_stored", "hi_stored", "lo_stored"))
        if router:
            (gwT, table_fill, slot_of, row_of, top_w) = router
            gw = sb("gw", [P, KD, E], F32)
            gw_parts = [sb("gw_hi", [P, KD, E], F32R), sb("gw_lo", [P, KD, E], F32R)]
            logits = sb("logits", [P, NT, E], F32)
            shifted = sb("shifted", [P, NT, E], F32)
            exps = sb("exps", [P, NT, E], F32)
            sums, rsums = sb("sums", [P, NT], F32), sb("rsums", [P, NT], F32)
            top = sb("top", [P, NT, K], F32)
            top_shifted = sb("top_shifted", [P, NT, K], F32)
            top_exp = sb("top_exp", [P, NT, K], F32)
            top_i = sb("top_i", [P, NT, K], U32)
            expert = sb("expert", [P, NT, K], F32)
            iota_e = sb("iota_e", [P, E], F32)
            spare = sb("spare", [P, NT, K], F32)
            earlier = sb("earlier", [P, P], BF16)
            ones = sb("ones", [P, P], BF16)
            onehot = sb("onehot", [P, NT, K, E], BF16)
            chosen = sb("chosen", [P, NT, E], BF16)
            chosen_f = sb("chosen_f", [P, NT, E], F32)
            before = sb("before", [P, NT, E], BF16)
            places = x_sb[:, :, :].rearrange("p t (k e) -> p t k e", e=E)
            pos, clipped, valid, slot_f = (sb(n, [P, NT, K], F32) for n in ("pos", "clipped", "valid", "slot_f"))
            fill = sb("fill", [P, P], I32)
            zero_row = sb("zero_row", [1, D], F32)
            logit_ps = ps("logit_ps", [P, NT, E], F32)
            pos_ps = ps("pos_ps", [P, NT, E], F32)
            (consts_loaded, gw_hi_done, gw_lo_done, logits_ready, routed, ones_set, shifted_done, exps_done,
             chosen_done, before_done, counted, fill_set, fill_stored, zero_set, zero_stored) = (
                sem(n) for n in ("consts_loaded", "gw_hi_done", "gw_lo_done", "logits_ready", "routed", "ones_set",
                                 "shifted_done", "exps_done", "chosen_done", "before_done", "counted", "fill_set",
                                 "fill_stored", "zero_set", "zero_stored"))
        block = ctx.enter_context(nc.Block())

        @block.sync
        def _(sp):
            for c in range(NC):
                sp.dma_start(x_sb[:, TPC * c:TPC * (c + 1), :],
                             x[CH * c:CH * (c + 1), :].rearrange("(t p) d -> p t d", p=P)).then_inc(x_loaded[c], 16)
            for c in range(NC):
                if xn_rows is not None:
                    sp.wait_ge(xn_done, TPC * (c + 1))
                    sp.dma_start(xn_rows[CH * c:CH * (c + 1), :].rearrange("(t p) d -> p t d", p=P),
                                 xn[:, TPC * c:TPC * (c + 1), :]).then_inc(rows_stored, 16)
                sp.wait_ge(hi_done, TPC * (c + 1))
                sp.dma_start(xnT[HI][c], f32(xT[HI][:, c])).then_inc(hi_stored, 16)
                sp.wait_ge(lo_done, TPC * (c + 1))
                sp.dma_start(xnT[LO][c], f32(xT[LO][:, c])).then_inc(lo_stored, 16)
            if xn_rows is not None:
                sp.wait_ge(rows_stored, 16 * NC)
            sp.wait_ge(hi_stored, 16 * NC)
            sp.wait_ge(lo_stored, 16 * NC)

        @block.scalar
        def _(act):
            act.dma_start(ident[:, :], consts["ident"]).then_inc(ident_loaded, 16)
            if router:
                act.dma_start(gw[:, :, :], gwT.rearrange("(k p) e -> p k e", p=P)).then_inc(consts_loaded, 16)
                act.dma_start(earlier[:, :], consts["earlier"]).then_inc(consts_loaded, 16)
                act.dma_start(iota_e[:, :], consts["iota_e"]).then_inc(consts_loaded, 16)
                act.dma_start(spare[:, :, :], consts["spare"]).then_inc(consts_loaded, 16)
            act.wait_ge(eps_set, 1)
            for c in range(NC):
                s = slice(TPC * c, TPC * (c + 1))
                act.wait_ge(moments_done, TPC * (c + 1))
                nc.scalar.activation(std[:, s], moments[:, s, 1], ACT.Sqrt, bias=eps[:, 0:1]).then_inc(std_done, 1)
            if router:
                act.wait_ge(consts_loaded, 64)
                nc.scalar.activation(gw_parts[HI][:, :, :], gw[:, :, :], ACT.Copy).then_inc(gw_hi_done, 1)
            for t in range(NT):
                act.wait_ge(transposed, t + 1)
                nc.scalar.activation(xT[HI][:, t // TPC, :, P * (t % TPC):P * (t % TPC + 1)], xT_ps[:, t % TURNS],
                                     ACT.Copy).then_inc(hi_done, 1)
            if router:
                act.wait_ge(shifted_done, 2)
                nc.scalar.activation(exps[:, :, :], shifted[:, :, :], ACT.Exp).then_inc(exps_done, 1)
                nc.scalar.activation(top_exp[:, :, :], top_shifted[:, :, :], ACT.Exp).then_inc(exps_done, 1)

        @block.tensor
        def _(pe):
            def logits(t):
                pe.wait_ge(lo_done, t + 1)
                pe.wait_ge(hi_done, t + 1)
                for n, (a, b) in enumerate(PRODUCTS):
                    for k in range(KD):
                        mm = nc.tensor.matmul(
                            logit_ps[:, t, :], xT[a][:, t // TPC, k, P * (t % TPC):P * (t % TPC + 1)],
                            gw_parts[b][:, k, :], start=(n == 0 and k == 0), stop=(n == 2 and k == KD - 1))
                mm.then_inc(logits_ready, 1)

            pe.wait_ge(ident_loaded, 16)
            for t in range(NT):
                if router and t == LOGITS_LAG:
                    pe.wait_ge(gw_hi_done, 1)
                    pe.wait_ge(gw_lo_done, 1)
                if router and t >= LOGITS_LAG:
                    logits(t - LOGITS_LAG)
                pe.wait_ge(xn_done, t + 1)
                if t >= TURNS:
                    pe.wait_ge(lo_done, t - TURNS + 1)
                for k in range(KD):
                    last = nc.tensor.transpose(xT_ps[:, t % TURNS, k, :], xn[:, t, P * k:P * (k + 1)], ident[:, :])
                last.then_inc(transposed, 1)
            if router:
                for t in range(NT - LOGITS_LAG, NT):
                    logits(t)
                pe.wait_ge(consts_loaded, 64)
                pe.wait_ge(ones_set, 1)
                pe.wait_ge(chosen_done, 1)
                pe.wait_ge(before_done, NT)
                for t in range(NT):
                    nc.tensor.matmul(pos_ps[:, t, :], earlier[:, :], chosen[:, t, :], start=True, stop=False)
                    last = nc.tensor.matmul(pos_ps[:, t, :], ones[:, :], before[:, t, :], start=False, stop=True)
                last.then_inc(counted, 1)

        @block.gpsimd
        def _(pool):
            if router:
                nc.gpsimd.memset(fill[:, :], T).then_inc(fill_set, 1)
                nc.gpsimd.memset(zero_row[:, :], 0.0).then_inc(zero_set, 1)
                pool.wait_ge(fill_set, 1)
                pool.dma_start(table_fill, fill[:, :]).then_inc(fill_stored, 16)
                pool.wait_ge(zero_set, 1)
                pool.dma_start(xn_rows[T:T + 1, :], zero_row[:, :]).then_inc(zero_stored, 16)
                pool.wait_ge(fill_stored, 16)
                pool.wait_ge(zero_stored, 16)

        @block.vector
        def _(dve):
            nc.vector.memset(eps[:, :], LN_EPS).then_inc(eps_set, 1)
            for c in range(NC):
                dve.wait_ge(x_loaded[c], 16)
                for t in range(TPC * c, TPC * (c + 1)):
                    nc.vector.bn_stats(stats[:, t, :], x_sb[:, t, :]).then_inc(stats_done, 1)
                for t in range(TPC * c, TPC * (c + 1)):
                    dve.wait_ge(stats_done, t + 1)
                    nc.vector.bn_aggr(moments[:, t, :], stats[:, t, :]).then_inc(moments_done, 1)
            for c in range(NC):
                s = slice(TPC * c, TPC * (c + 1))
                dve.wait_ge(std_done, c + 1)
                nc.vector.reciprocal(rstd[:, s], std[:, s]).then_inc(rstd_done, 1)
            if router:
                dve.wait_ge(gw_hi_done, 1)
                nc.vector.tensor_tensor(gw_parts[LO][:, :, :], gw[:, :, :], f32(gw_parts[HI][:, :, :]),
                                        ALU.subtract).then_inc(gw_lo_done, 1)
            for t in range(NT + 2):
                if t < NT:
                    dve.wait_ge(rstd_done, t // TPC + 1)
                    nc.vector.tensor_scalar(xn[:, t, :], x_sb[:, t, :], moments[:, t, 0:1], rstd[:, t:t + 1],
                                            ALU.subtract, ALU.mult).then_inc(xn_done, 1)
                if t >= 2:
                    u = t - 2
                    dve.wait_ge(hi_done, u + 1)
                    here = (slice(None), u // TPC, slice(None), slice(P * (u % TPC), P * (u % TPC + 1)))
                    nc.vector.tensor_tensor(xT[LO][here], xT_ps[:, u % TURNS], f32(xT[HI][here]),
                                            ALU.subtract).then_inc(lo_done, 1)
            if not router:
                return
            nc.vector.memset(ones[:, :], 1.0).then_inc(ones_set, 1)
            steps = [0]

            def step(ins):
                ins.then_inc(routed, 1)
                steps[0] += 1

            def steps_done():
                dve.wait_ge(routed, steps[0])

            dve.wait_ge(logits_ready, NT)
            step(nc.vector.tensor_copy(logits[:, :, :], logit_ps[:, :, :]))
            steps_done()
            for t in range(NT):
                step(nc.vector.max(top[:, t, :], logits[:, t, :]))
            steps_done()
            nc.vector.tensor_tensor(shifted[:, :, :], logits[:, :, :], top[:, :, 0:1].broadcast_to([P, NT, E]),
                                    ALU.subtract).then_inc(shifted_done, 1)
            nc.vector.tensor_tensor(top_shifted[:, :, :], top[:, :, :], top[:, :, 0:1].broadcast_to([P, NT, K]),
                                    ALU.subtract).then_inc(shifted_done, 1)
            for t in range(NT):
                step(nc.vector.max_index(top_i[:, t, :], top[:, t, :], logits[:, t, :]))
            steps_done()
            step(nc.vector.tensor_copy(expert[:, :, :], top_i[:, :, :]))
            steps_done()
            dve.wait_ge(consts_loaded, 64)
            step(nc.vector.tensor_tensor(
                onehot[:, :, :, :].rearrange("p t k e -> p (t k) e"),
                iota_e[:, :].unsqueeze(1).broadcast_to([P, NT * K, E]),
                expert[:, :, :].rearrange("p t k -> p (t k)").unsqueeze(2).broadcast_to([P, NT * K, E]),
                ALU.is_equal))
            steps_done()
            step(nc.vector.tensor_reduce(chosen_f[:, :, :], onehot[:, :, :, :].rearrange("p t k e -> p t e k"),
                                         AX_X, ALU.add))
            steps_done()
            nc.vector.tensor_copy(chosen[:, :, :], chosen_f[:, :, :]).then_inc(chosen_done, 1)
            nc.vector.memset(before[:, 0, :], 0.0).then_inc(before_done, 1)
            dve.wait_ge(chosen_done, 1)
            for t in range(1, NT):
                dve.wait_ge(before_done, t)
                nc.vector.tensor_tensor(before[:, t, :], before[:, t - 1, :], chosen[:, t - 1, :],
                                        ALU.add).then_inc(before_done, 1)
            dve.wait_ge(counted, 1)
            step(nc.vector.tensor_tensor(places, onehot[:, :, :, :],
                                         pos_ps[:, :, :].unsqueeze(2).broadcast_to([P, NT, K, E]), ALU.mult))
            steps_done()
            step(nc.vector.tensor_reduce(pos[:, :, :], places, AX_X, ALU.add))
            steps_done()
            step(nc.vector.tensor_scalar(valid[:, :, :], pos[:, :, :], float(CAP), None, ALU.is_lt))
            step(nc.vector.tensor_scalar(clipped[:, :, :], pos[:, :, :], float(CAP - 1), None, ALU.min))
            steps_done()
            step(nc.vector.scalar_tensor_tensor(slot_f[:, :, :], expert[:, :, :], float(CAP), clipped[:, :, :],
                                                ALU.mult, ALU.add))
            steps_done()
            step(nc.vector.tensor_copy(row_of[:, :, :], slot_f[:, :, :]))
            step(nc.vector.tensor_tensor(clipped[:, :, :], slot_f[:, :, :], spare[:, :, :], ALU.subtract))
            steps_done()
            step(nc.vector.tensor_tensor(clipped[:, :, :], clipped[:, :, :], valid[:, :, :], ALU.mult))
            steps_done()
            step(nc.vector.tensor_tensor(slot_of[:, :, :], clipped[:, :, :], spare[:, :, :], ALU.add))
            dve.wait_ge(exps_done, 2)
            step(nc.vector.tensor_reduce(sums[:, :], exps[:, :, :], AX_X, ALU.add))
            steps_done()
            step(nc.vector.reciprocal(rsums[:, :], sums[:, :]))
            step(nc.vector.tensor_tensor(top_exp[:, :, :], top_exp[:, :, :], valid[:, :, :], ALU.mult))
            steps_done()
            step(nc.vector.tensor_tensor(top_w[:, :, :], top_exp[:, :, :],
                                         rsums[:, :].unsqueeze(2).broadcast_to([P, NT, K]), ALU.mult))

FF = 2048
FT = FF // P
QEPS = 1e-8
HALF_UP, PRODUCT, BOUND, LESS_BOUND, SCALES = 3, 4, 5, 8, 11
QKV_OUT = 3 * NG

def qkv_phase(nc, consts, xnT, Wqkv, bqk, bv, qk_parts, v_rows, ffn_wT, scales):
    with ExitStack() as ctx:
        sb = lambda name, shape, dt: ctx.enter_context(nc.sbuf_tensor(f"qkv_{name}", shape, dt))
        sem = ctx.enter_context(semaphores(nc, "qkv"))
        w = sb("w", [P, KD, 3 * D], F32)
        w_parts = [sb("w_hi", [P, KD, 3 * D], F32R), sb("w_lo", [P, KD, 3 * D], F32R)]
        xc = sb("xc", [P, 2, 2, KD, CH], F32R)
        out = sb("out", [P, 4, 2, CH], F32R)
        v_out = sb("v_out", [P, TPC, D], F32)
        bias = sb("bias", [P, 2 * NG], F32)
        v_bias = sb("v_bias", [P, D], F32)
        acc = ctx.enter_context(nc.psum_tensor("qkv_acc", [P, 4, CH], F32))
        fw = sb("fw", [P, 3, FF], F32)
        fw_sum, fw_total = sb("fw_sum", [P, 3], F32), sb("fw_total", [P, 3], F32)
        ones = sb("ones", [P, P], F32)
        sum_ps = ctx.enter_context(nc.psum_tensor("qkv_sum_ps", [P, CH], F32))

        w_loaded = [sem(f"w_loaded{k}") for k in range(KD)]
        bias_loaded, w_hi_done, w_lo_done = sem("bias_loaded"), sem("w_hi_done"), sem("w_lo_done")
        xc_loaded = [sem(f"xc_loaded{b}") for b in range(2)]
        acc_ready, acc_free, hi_done, lo_done, v_done = (
            sem(n) for n in ("acc_ready", "acc_free", "hi_done", "lo_done", "v_done"))
        out_stored = [sem(f"out_stored{b}") for b in range(4)]
        v_stored = [sem(f"v_stored{b}") for b in range(TPC)]
        fw_loaded = [sem(f"fw_loaded{w_}") for w_ in range(3)]
        fw_read, fw_added, ones_set, summed, scale_step = (
            sem(n) for n in ("fw_read", "fw_added", "ones_set", "summed", "scale_step"))
        block = ctx.enter_context(nc.Block())

        @block.sync
        def _(sp):
            def load(chunk, b):
                for part in (HI, LO):
                    sp.dma_start(f32(xc[:, b, part]), xnT[part][chunk]).then_inc(xc_loaded[b], 16)

            for k in range(KD):
                sp.dma_start(w[:, k, :], Wqkv[P * k:P * (k + 1), :]).then_inc(w_loaded[k], 16)
                if k % 2:
                    load(k // 2, k // 2)

            def store(chunk, n, b):
                sp.wait_ge(fw_read, 3 * (n + 1))
                for w_ in range(3):
                    src = (ffn_wT[w_][bass.ds(n * P, P), :] if w_ < 2 else
                           ffn_wT[w_][bass.ds(n * CH, CH), :].rearrange("(f p) d -> p f d", p=P))
                    dst = fw[:, w_] if w_ < 2 else fw[:, w_].rearrange("p (f d) -> p f d", d=D)
                    sp.dma_start(dst, src).then_inc(fw_loaded[w_], 16)
                for m in range(2 * NG):
                    sp.wait_ge(lo_done, n * 2 * NG + m + 1)
                    sp.dma_start(qk_parts[m // NG, m % NG, :, :, bass.ds(chunk * CH, CH)].rearrange("a p t -> p a t"),
                                 f32(out[:, m % 4])).then_inc(out_stored[m % 4], 16)
                for t in range(TPC):
                    sp.wait_ge(v_done, n * TPC + t + 1)
                    sp.dma_start(v_rows[bass.ds(chunk * CH + t * P, P), :], v_out[:, t]).then_inc(v_stored[t], 16)

            with sp.Fori(0, NC // 2 - 1) as i:
                for b in range(2):
                    n = 2 * i + b
                    store(n, n, b)
                    sp.wait_ge(acc_ready, (n + 1) * QKV_OUT)
                    load(n + 2, b)
            for b in range(2):
                store(NC - 2 + b, NC - 2 + b, b)
            for b in range(4):
                sp.wait_ge(out_stored[b], 16 * (1 + 2 * NC))
                sp.wait_ge(v_stored[b], 16 * (1 + NC))

        @block.tensor
        def _(pe):
            with pe.Fori(0, NC // 2) as i:
                for b in range(2):
                    n = 2 * i + b
                    pe.wait_ge(xc_loaded[b], 32 * (i + 1))
                    for j in range(QKV_OUT):
                        if j % KD == 0:
                            pe.wait_ge(w_lo_done, KD)
                        pe.wait_ge(acc_free, n * QKV_OUT + j + 1)
                        for q, (wa, xa) in enumerate(PRODUCTS):
                            for k in range(KD):
                                first, last = q == 0 and k == 0, q == 2 and k == KD - 1
                                if j < 2 * NG:
                                    mm = nc.tensor.matmul(acc[:, j % 4], w_parts[wa][:, k, P * j:P * (j + 1)],
                                                          xc[:, b, xa, k, :], start=first, stop=last)
                                else:
                                    t = j - 2 * NG
                                    mm = nc.tensor.matmul(acc[:, j % 4], xc[:, b, xa, k, P * t:P * (t + 1)],
                                                          w_parts[wa][:, k, 2 * D:3 * D], start=first, stop=last)
                        mm.then_inc(acc_ready, 1)
            pe.wait_ge(ones_set, 1)
            pe.wait_ge(fw_added, 1 + NC)
            nc.tensor.matmul(sum_ps[:, 0:3], ones[:, :], fw_total[:, :], start=True, stop=True).then_inc(summed, 1)

        @block.scalar
        def _(act):
            act.dma_start(bias[:, :], bqk).then_inc(bias_loaded, 16)
            act.dma_start(v_bias[:, :], bv.unsqueeze(0).broadcast_to([P, D])).then_inc(bias_loaded, 16)
            for b in range(4):
                act.sem_inc(out_stored[b], 16)
            for k in range(KD):
                act.wait_ge(w_loaded[k], 16)
                nc.scalar.activation(w_parts[HI][:, k, :], w[:, k, :], ACT.Copy).then_inc(w_hi_done, 1)
            act.wait_ge(bias_loaded, 32)
            with act.Fori(0, NC) as n:
                for m in range(2 * NG):
                    act.wait_ge(acc_ready, n * QKV_OUT + m + 1)
                    act.wait_ge(out_stored[m % 4], n * 32 + 16 * (m // 4) + 16)
                    nc.scalar.activation(out[:, m % 4, HI], acc[:, m % 4], ACT.Identity,
                                         bias=bias[:, m:m + 1]).then_inc(hi_done, 1)

        @block.vector
        def _(dve):
            dve.sem_inc(acc_free, 4)
            dve.sem_inc(fw_read, 3)
            nc.vector.memset(ones[:, :], 1.0).then_inc(ones_set, 1)
            nc.vector.memset(fw_total[:, :], 0.0).then_inc(fw_added, 1)
            for b in range(TPC):
                dve.sem_inc(v_stored[b], 16)
            for k in range(KD):
                dve.wait_ge(w_hi_done, k + 1)
                nc.vector.tensor_tensor(w_parts[LO][:, k, :], w[:, k, :], f32(w_parts[HI][:, k, :]),
                                        ALU.subtract).then_inc(w_lo_done, 1)
            dve.wait_ge(bias_loaded, 32)
            with dve.Fori(0, NC) as n:
                for m in range(2 * NG):
                    dve.wait_ge(hi_done, n * 2 * NG + m + 1)
                    nc.vector.scalar_tensor_tensor(out[:, m % 4, LO], acc[:, m % 4], bias[:, m:m + 1],
                                                   f32(out[:, m % 4, HI]), ALU.add, ALU.subtract).then_inc(lo_done, 1)
                    dve.wait_ge(lo_done, n * 2 * NG + m + 1)
                    dve.sem_inc(acc_free, 1)
                    if m >= 2 * NG - 3:
                        w_ = m - 2 * NG + 3
                        dve.wait_ge(fw_loaded[w_], n * 16 + 16)
                        nc.vector.tensor_reduce(fw_sum[:, w_:w_ + 1], fw[:, w_], AX_X, ALU.add,
                                                apply_absolute_value=True).then_inc(fw_read, 1)
                dve.wait_ge(fw_read, 3 * n + 6)
                dve.wait_ge(fw_added, n + 1)
                nc.vector.tensor_tensor(fw_total[:, :], fw_total[:, :], fw_sum[:, :], ALU.add).then_inc(fw_added, 1)
                for t in range(TPC):
                    dve.wait_ge(acc_ready, n * QKV_OUT + 2 * NG + t + 1)
                    dve.wait_ge(v_stored[t], n * 16 + 16)
                    nc.vector.tensor_tensor(v_out[:, t], acc[:, t], v_bias[:, :], ALU.add).then_inc(v_done, 1)
                    dve.wait_ge(v_done, n * TPC + t + 1)
                    dve.sem_inc(acc_free, 1)
            dve.wait_ge(summed, 1)
            nc.vector.tensor_scalar(scales[:, 0:3], sum_ps[:, 0:3], 1.0 / (D * FF), QEPS, ALU.mult,
                                    ALU.add).then_inc(scale_step, 1)
            dve.wait_ge(scale_step, 1)
            nc.vector.tensor_scalar(scales[:, BOUND:BOUND + 3], scales[:, 0:3], 0.5, None, ALU.mult).then_inc(scale_step, 1)
            nc.vector.tensor_scalar(scales[:, LESS_BOUND:LESS_BOUND + 3], scales[:, 0:3], -0.5, None, ALU.mult).then_inc(scale_step, 1)
            nc.vector.tensor_scalar(scales[:, HALF_UP:HALF_UP + 1], scales[:, 0:1], 0.5, None, ALU.mult).then_inc(scale_step, 1)
            dve.wait_ge(scale_step, 4)
            nc.vector.scalar_tensor_tensor(scales[:, PRODUCT:PRODUCT + 1], scales[:, HALF_UP:HALF_UP + 1], scales[:, 1:2],
                                           scales[:, 2:3], ALU.mult, ALU.mult).then_inc(scale_step, 1)

TQ = L // P
SCALE = HD ** -0.5
PAIRS = HPG // 2
STEPS = [(half, kb) for half in range(L // CH) for kb in range((half + 1) * CH // P)]
NSTEPS = len(STEPS)
PIECES = [(j, a, min(a + CH, P * (j + 1))) for j in range(TQ) for a in range(0, P * (j + 1), CH)]
NPIECES = HPG * len(PIECES)
FIRST_TOP_STEP, TOPS_PER_STEP = 4, 8
QROWS = 3 * HD

def attention_phase(nc, consts, qk_parts, v_rows, attnT, background):
    with ExitStack() as ctx:
        sb = lambda name, shape, dt: ctx.enter_context(nc.sbuf_tensor(f"att_{name}", shape, dt))
        ps = lambda name, shape, dt: ctx.enter_context(nc.psum_tensor(f"att_{name}", shape, dt))
        sem = ctx.enter_context(semaphores(nc, "att"))
        q, k = (sb(n, [P, 2, HPG, L], F32R) for n in ("q", "k"))
        v = sb("v", [P, 2, TQ, P], F32)
        ones = sb("ones", [P, HD], F32)
        probs = sb("probs", [P, 2, HPG, CH], F32)
        ident, ident_b = sb("ident", [P, P], F32), sb("ident_b", [P, P], BF16)
        mask, maskT = sb("mask", [P, P], BF16), sb("maskT", [P, P], BF16)
        top = sb("top", [P, HPG, TQ], F32)
        top_rest = sb("top_rest", [P, HPG, TQ // 2], F32)
        less_top = sb("less_top", [HPG * TQ, 2, P], F32R)
        sums, total = sb("sums", [P, 2, L], F32), sb("total", [P, 2, L], F32)
        shares, out = sb("shares", [P, L], F32), sb("out", [P, 2, L], F32)
        s_ps = ps("s_ps", [P, 2, CH], F32)
        st_ps = ps("st_ps", [P, PAIRS, 2, CH], F32)
        o_ps, r_ps = ps("o_ps", [P, CH], F32), ps("r_ps", [P, CH], F32)

        consts_loaded, ones_set = sem("consts_loaded"), sem("ones_set")
        loaded = [[sem(f"loaded{b}{pair}") for pair in range(PAIRS)] for b in range(2)]
        v_loaded, top_loaded, stored = ([sem(f"{n}{b}") for b in range(2)] for n in ("v_loaded", "top_loaded", "stored"))
        (scores_ready, top_taken, top_done, top_turned, less_top_done, scoresT_ready, probs_done, pv_done, taken,
         recip_done, out_done) = (sem(n) for n in (
             "scores_ready", "top_taken", "top_done", "top_turned", "less_top_done", "scoresT_ready", "probs_done",
             "pv_done", "taken", "recip_done", "out_done"))
        beside = background(ctx, sem)
        block = ctx.enter_context(nc.Block())

        def turns(eng, visit):
            with eng.Fori(0, NG - 1) as g:
                for b in range(2):
                    visit(g, b, 2 * g + b, True)
            for b in range(2):
                visit(NG - 1, b, 2 * (NG - 1) + b, b == 0)

        def width(n):
            half, kb = STEPS[n]
            first = max(CH * half, P * kb)
            return first, CH * (half + 1) - first

        def pieces_beside(n):
            first = max(n - FIRST_TOP_STEP, 0) * TOPS_PER_STEP
            return range(first, min(first + TOPS_PER_STEP, NPIECES)) if n >= FIRST_TOP_STEP else range(0)

        LAST_TOP_STEP = FIRST_TOP_STEP + NPIECES // TOPS_PER_STEP - 1

        @block.sync
        def _(sp):
            def load_stacks(g, b):
                for pair in range(PAIRS):
                    heads = slice(2 * pair, 2 * pair + 2)
                    for which, (dst, parts) in enumerate(((q, (HI, HI, LO)), (k, (HI, LO, HI)))):
                        for r, part in enumerate(parts):
                            src = qk_parts[which, bass.ds(g, 1), part, 2 * HD * pair:2 * HD * (pair + 1), L * b:L * (b + 1)]
                            sp.dma_start(f32(dst[HD * r:HD * (r + 1), b, heads, :]),
                                         src.rearrange("g (i h) t -> h (g i) t", h=HD)).then_inc(loaded[b][pair], 16)

            def load_v(g, b):
                sp.dma_start(v[:, b], v_rows[L * b:L * (b + 1), bass.ds(g * P, P)].rearrange(
                    "(s p) d -> p s d", p=P)).then_inc(v_loaded[b], 16)

            def load_top(b, turn):
                sp.wait_ge(less_top_done, turn + 1)
                sp.dma_start(f32(q[QROWS:QROWS + 1, b, :, :]).rearrange("a i (j p) -> a (i j) p", p=P),
                             f32(less_top[:, b, :])).then_inc(top_loaded[b], 16)

            def visit(g, b, turn, more):
                beside["load"](sp, g, b, turn)
                if more:
                    load_top(1 - b, turn + 1)
                if g is not NG - 1:
                    sp.wait_ge(scoresT_ready, (turn + 1) * NSTEPS * PAIRS)
                    load_stacks(g + 1, b)
                sp.wait_ge(out_done, turn + 3)
                sp.dma_start(attnT[bass.ds(g, 1), :, L * b:L * (b + 1)].rearrange("g p t -> (g p) t"),
                             out[:, b]).then_inc(stored[b], 16)
                if g is not NG - 1:
                    load_v(g + 1, b)
                beside["store"](sp, g, b, turn)

            load_stacks(0, 0)
            load_v(0, 0)
            load_stacks(0, 1)
            load_v(0, 1)
            load_top(0, 0)
            turns(sp, visit)
            for b in range(2):
                sp.wait_ge(stored[b], 16 * (1 + NG))
            beside["finish"](sp)

        @block.tensor
        def _(pe):
            def piece(b, turn, u):
                i, (j, a, e) = u // len(PIECES), PIECES[u % len(PIECES)]
                pe.wait_ge(top_taken, turn * NPIECES + u + 1)
                diagonal = e == P * (j + 1)
                mm = nc.tensor.matmul(s_ps[:, u % 2, 0:e - a], q[0:QROWS, b, i, P * j:P * (j + 1)],
                                      k[0:QROWS, b, i, a:e], start=True, stop=not diagonal)
                if diagonal:
                    mm = nc.tensor.matmul(s_ps[:, u % 2, e - a - P:e - a], ident_b[:, :], mask[:, :], start=False,
                                          stop=True)
                mm.then_inc(scores_ready, 1)

            def turn_top(turn):
                pe.wait_ge(top_done, turn + 1)
                nc.tensor.transpose(s_ps[0:HPG * TQ, 0, 0:P], top[:, :, :].rearrange("p i j -> p (i j)"),
                                    ident[:, :]).then_inc(top_turned, 1)

            def scoresT(b, turn, n, pair):
                half, kb = STEPS[n]
                first, w = width(n)
                pe.wait_ge(probs_done, turn * NSTEPS * PAIRS + PAIRS * n + pair + 1)
                diagonal = P * kb == first
                for h in range(2):
                    i = 2 * pair + h
                    mm = nc.tensor.matmul(st_ps[:, pair, h, 0:w], k[0:QROWS + 1, b, i, P * kb:P * (kb + 1)],
                                          q[0:QROWS + 1, b, i, first:first + w], start=True, stop=not diagonal)
                    if diagonal:
                        mm = nc.tensor.matmul(st_ps[:, pair, h, 0:P], ident_b[:, :], maskT[:, :], start=False, stop=True)
                mm.then_inc(scoresT_ready, 1)

            def values(b, turn, n, which):
                half, kb = STEPS[n]
                first, w = width(n)
                if which == 0:
                    pe.wait_ge(probs_done, turn * NSTEPS * PAIRS + PAIRS * (n + 1) + 2)
                if kb == 0:
                    pe.wait_ge(taken, turn * 4 + 2 * half + which + 1)
                for i in range(HPG):
                    c = slice(HD * i, HD * (i + 1))
                    mm = nc.tensor.matmul((o_ps, r_ps)[which][c, first - CH * half:CH],
                                          v[:, b, kb, c] if which == 0 else ones[:, :],
                                          probs[:, n % 2, i, 0:w], start=(kb == 0), stop=(first + P == CH * (half + 1)))
                mm.then_inc(pv_done, 1)

            def visit(g, b, turn, more):
                pe.wait_ge(top_loaded[b], 16 * (g + 2))
                for n in range(NSTEPS + 1):
                    tops = list(pieces_beside(n)) if more and n < NSTEPS else []
                    part = (len(tops) + 3) // 4
                    if n < NSTEPS:
                        scoresT(b, turn, n, 0)
                    for s in range(4):
                        if s == 0 and tops and tops[0] % (2 * len(PIECES)) == 0:
                            pair = tops[0] // (2 * len(PIECES))
                            pe.wait_ge(loaded[1 - b][pair], 96 * (g + b + 1))
                            if pair == 0:
                                pe.wait_ge(less_top_done, turn + 1)
                        for u in tops[s * part:(s + 1) * part]:
                            piece(1 - b, turn + 1, u)
                        if s == 0 and n:
                            if n == 1:
                                pe.wait_ge(v_loaded[b], 16 * (g + 1))
                            values(b, turn, n - 1, 0)
                        if s == 0 and more and n == LAST_TOP_STEP + 1:
                            turn_top(turn + 1)
                        if s == 1 and n < NSTEPS:
                            scoresT(b, turn, n, 1)
                        if s == 2 and n:
                            values(b, turn, n - 1, 1)

            pe.wait_ge(consts_loaded, 64)
            pe.wait_ge(ones_set, 3)
            for u in range(NPIECES):
                if u % (2 * len(PIECES)) == 0:
                    pe.wait_ge(loaded[0][u // (2 * len(PIECES))], 96)
                piece(0, 0, u)
            turn_top(0)
            turns(pe, visit)

        @block.scalar
        def _(act):
            act.dma_start(ident[:, :], consts["ident"]).then_inc(consts_loaded, 16)
            act.dma_start(ident_b[:, :], consts["ident_b"]).then_inc(consts_loaded, 16)
            act.dma_start(mask[:, :], consts["mask"]).then_inc(consts_loaded, 16)
            act.dma_start(maskT[:, :], consts["maskT"]).then_inc(consts_loaded, 16)

            def take(b, turn, half):
                for which, (dst, src) in enumerate(((total, o_ps), (sums, r_ps))):
                    act.wait_ge(pv_done, turn * NSTEPS * 2 + 2 * (4 if half == 0 else NSTEPS) - 1 + which + 4)
                    if half == 0:
                        act.wait_ge(out_done, turn + 1)
                    nc.scalar.activation(dst[:, b, CH * half:CH * (half + 1)], src[:, :], ACT.Copy).then_inc(taken, 1)

            def visit(g, b, turn, more):
                for n in range(NSTEPS):
                    first, w = width(n)
                    for pair in range(PAIRS):
                        act.wait_ge(scoresT_ready, turn * NSTEPS * PAIRS + PAIRS * n + pair + 1)
                        if pair == 0:
                            act.wait_ge(pv_done, turn * NSTEPS * 2 + 2 * n + 2)
                        nc.scalar.activation(probs[:, n % 2, 2 * pair:2 * pair + 2, 0:w], st_ps[:, pair, :, 0:w],
                                             ACT.Exp, scale=SCALE).then_inc(probs_done, 1)
                    if n == 4:
                        take(b, turn, 0)
                take(b, turn, 1)
            turns(act, visit)

        @block.vector
        def _(dve):
            for b in range(2):
                nc.vector.memset(f32(k[QROWS:QROWS + 1, b, :, :]), 1.0).then_inc(ones_set, 1)
            nc.vector.memset(ones[:, :], 1.0).then_inc(ones_set, 1)
            beside["start"](dve)
            dve.sem_inc(top_taken, 2)
            dve.sem_inc(probs_done, PAIRS)
            dve.sem_inc(pv_done, 4)
            dve.sem_inc(taken, 2)
            dve.sem_inc(out_done, 2)
            for b in range(2):
                dve.sem_inc(stored[b], 16)
                dve.sem_inc(top_loaded[b], 16)

            def maximum(turn, u):
                i, (j, a, e) = u // len(PIECES), PIECES[u % len(PIECES)]
                dve.wait_ge(scores_ready, turn * NPIECES + u + 1)
                dst = top[:, i, j:j + 1] if a == 0 else top_rest[:, i, j - TQ // 2:j - TQ // 2 + 1]
                nc.vector.reduce_max(dst, s_ps[:, u % 2, 0:e - a], AX_X).then_inc(top_taken, 1)

            def finish_top(b, turn, loads):
                dve.wait_ge(top_taken, (turn + 1) * NPIECES + 2)
                nc.vector.tensor_tensor(top[:, :, TQ // 2:TQ], top[:, :, TQ // 2:TQ], top_rest[:, :, :],
                                        ALU.max).then_inc(top_done, 1)
                dve.wait_ge(top_turned, turn + 1)
                dve.wait_ge(top_loaded[b], 16 * loads + 16)
                nc.vector.tensor_scalar(less_top[:, b, :], s_ps[0:HPG * TQ, 0, 0:P], -1.0, None,
                                        ALU.mult).then_inc(less_top_done, 1)

            def visit(g, b, turn, more):
                if more:
                    for u in range(NPIECES):
                        maximum(turn + 1, u)
                    finish_top(1 - b, turn + 1, g + b)
                beside["ternary"](dve, g, b, turn)
                dve.wait_ge(taken, turn * 4 + 6)
                dve.wait_ge(out_done, turn + 2)
                nc.vector.reciprocal(shares[:, :], sums[:, b, :]).then_inc(recip_done, 1)
                dve.wait_ge(recip_done, turn + 1)
                dve.wait_ge(stored[b], 16 * (g + 1))
                nc.vector.tensor_tensor(out[:, b, :], total[:, b, :], shares[:, :], ALU.mult).then_inc(out_done, 1)

            for u in range(NPIECES):
                maximum(0, u)
            finish_top(0, 0, 0)
            turns(dve, visit)

        @block.gpsimd
        def _(pool):
            beside["scatter"](pool)

KF = F // P
HALVES = CAP // P

def attention_background(nc, consts, table, slot_of, ffn_wT, scales, tern_d):
    def prepare(ctx, sem):
        sb = lambda name, shape, dt: ctx.enter_context(nc.sbuf_tensor(f"back_{name}", shape, dt))
        EIGHTH = KD * FF // (2 * NG)
        tokens = sb("tokens", [P, NT], I32)
        w, tern = sb("w", [P, 2, 3, EIGHTH], F32), sb("tern", [P, 2, 3, EIGHTH], F32)
        below = sb("below", [P, 3, EIGHTH], F32)
        tokens_loaded, scattered, below_done, tern_done = (
            sem(f"back_{n}") for n in ("tokens_loaded", "scattered", "below_done", "tern_done"))
        w_loaded, tern_stored = ([sem(f"back_{n}{b}") for b in range(2)] for n in ("w_loaded", "tern_stored"))

        def scatter(pool):
            pool.dma_start(tokens[:, :], consts["tokens"]).then_inc(tokens_loaded, 16)
            pool.wait_ge(tokens_loaded, 16)
            for t in range(NT):
                for k in range(K):
                    pool.indirect_dma_start(table, bass.IndirectOffsetOnAxis(ap=slot_of[:, t, k:k + 1], axis=0),
                                            tokens[:, t:t + 1], None).then_inc(scattered, 16)
            pool.wait_ge(scattered, 16 * NT * K)

        def load(sp, g, b, turn):
            sp.wait_ge(tern_done, 3 * turn + 3)
            for n in range(2):
                sp.dma_start(w[:, b, n], ffn_wT[n][bass.ds(g * P, P), EIGHTH * b:EIGHTH * (b + 1)]).then_inc(w_loaded[b], 16)
            sp.dma_start(w[:, b, 2].rearrange("p (f d) -> p f d", d=D), ffn_wT[2][bass.ds(g * 4 * P + 2 * P * b, 2 * P), :].rearrange(
                "(f p) d -> p f d", p=P)).then_inc(w_loaded[b], 16)

        def store(sp, g, b, turn):
            sp.wait_ge(tern_done, 3 * turn + 9)
            sp.dma_start(tern_d[bass.ds(turn * 2, 2), :, 2, :].rearrange("f p d -> p f d"),
                         tern[:, b, 2].rearrange("p (f d) -> p f d", d=D)).then_inc(tern_stored[b], 16)
            for n in range(2):
                sp.dma_start(tern_d[FT // 2 * b:FT // 2 * (b + 1), :, n, bass.ds(g * P, P)].rearrange("f p j -> p f j"),
                             tern[:, b, n].rearrange("p (f j) -> p f j", j=P)).then_inc(tern_stored[b], 16)

        def finish(sp):
            for b in range(2):
                sp.wait_ge(tern_stored[b], 48 * (1 + NG))

        def start(dve):
            dve.sem_inc(tern_done, 6)
            for b in range(2):
                dve.sem_inc(tern_stored[b], 48)

        def ternary(dve, g, b, turn):
            dve.wait_ge(w_loaded[b], 48 * (g + 1))
            for n in range(3):
                dve.wait_ge(tern_done, 3 * turn + n + 4)
                nc.vector.tensor_scalar(below[:, n], w[:, b, n], scales[:, LESS_BOUND + n:LESS_BOUND + n + 1], None,
                                        ALU.is_lt).then_inc(below_done, 1)
            dve.wait_ge(tern_stored[b], 48 * (g + 1))
            for n in range(3):
                dve.wait_ge(below_done, 3 * turn + n + 1)
                nc.vector.scalar_tensor_tensor(tern[:, b, n], w[:, b, n], scales[:, BOUND + n:BOUND + n + 1], below[:, n],
                                               ALU.is_gt, ALU.subtract).then_inc(tern_done, 1)
        return {"scatter": scatter, "load": load, "store": store, "finish": finish, "start": start, "ternary": ternary}
    return prepare

def experts_phase(nc, consts, xn_rows, table_rows, w_gate, w_up, w_down, y_rows):
    with ExitStack() as ctx:
        sb = lambda name, shape, dt: ctx.enter_context(nc.sbuf_tensor(f"moe_{name}", shape, dt))
        ps = lambda name, shape, dt: ctx.enter_context(nc.psum_tensor(f"moe_{name}", shape, dt))
        sem = ctx.enter_context(semaphores(nc, "moe"))
        tbl = sb("tbl", [P, P], I32)
        tbl_f = sb("tbl_f", [P, P], F32)
        tokens_of = sb("tokens_of", [P, E * HALVES], U32)
        index = sb("index", [P, 2, HALVES], U32)
        ident = sb("ident", [P, P], F32)
        gu_in = sb("gu_in", [P, 2, 2, KD, F], F32)
        gu_hi, gu_lo = sb("gu_hi", [P, 2, 2, KD, F], F32R), sb("gu_lo", [P, 2, 2, KD, F], F32R)
        d_in = sb("d_in", [P, 2, KF, D], F32)
        d_hi, d_lo = sb("d_hi", [P, 2, KF, D], F32R), sb("d_lo", [P, 2, KF, D], F32R)
        xg = sb("xg", [P, 2, HALVES, D], F32)
        xt_hi, xt_lo = sb("xt_hi", [P, 2, KD, CAP], F32R), sb("xt_lo", [P, 2, KD, CAP], F32R)
        act_g = sb("act_g", [P, 2, KF, CAP], F32)
        h = sb("h", [P, 2, KF, CAP], F32)
        h_hi, h_lo = sb("h_hi", [P, 2, KF, CAP], F32R), sb("h_lo", [P, 2, KF, CAP], F32R)
        y = sb("y", [P, 2, HALVES, D], F32)
        xt_ps = ps("xt_ps", [P, KD, CAP], F32)
        gu_ps = ps("gu_ps", [P, 2, 2, KF, CAP], F32)
        y_ps = ps("y_ps", [P, HALVES, D], F32)

        consts_loaded, tbl_f_done, tbl_turned, tokens_done, index_done, gathers_begun = (
            sem(n) for n in ("consts_loaded", "tbl_f_done", "tbl_turned", "tokens_done", "index_done",
                             "gathers_begun"))
        gu_loaded, d_loaded, gathered, y_stored = ([sem(f"{n}{b}") for b in range(2)] for n in (
            "gu_loaded", "d_loaded", "gathered", "y_stored"))
        (gu_hi_done, gu_lo_done, d_hi_done, d_lo_done, xt_ready, xt_hi_done, xt_lo_done, gate_ready, up_ready,
         act_done, h_done, h_hi_done, h_lo_done, y_ready, y_done) = (
            sem(n) for n in ("gu_hi_done", "gu_lo_done", "d_hi_done", "d_lo_done", "xt_ready", "xt_hi_done",
                             "xt_lo_done", "gate_ready", "up_ready", "act_done", "h_done", "h_hi_done",
                             "h_lo_done", "y_ready", "y_done"))
        block = ctx.enter_context(nc.Block())

        def each_expert(eng, visit):
            for b in range(2):
                visit(b, b, 0)
            with eng.Fori(1, E // 2 - 1) as i:
                for b in range(2):
                    visit(2 * i + b, b, i)
            for b in range(2):
                visit(E - 2 + b, b, E // 2 - 1)

        def known(e):
            return isinstance(e, int)

        def exists(e, ahead):
            return not known(e) or 0 <= e + ahead < E

        def wait(eng, sem_, value):
            if not known(value) or value > 0:
                eng.wait_ge(sem_, value)

        @block.sync
        def _(sp):
            def load_gu(e, b):
                for w, src in enumerate((w_gate, w_up)):
                    sp.dma_start(gu_in[:, b, w], src[bass.ds(e, 1)].rearrange("e (k p) f -> p (e k) f", p=P)
                                 ).then_inc(gu_loaded[b], 16)

            def load_d(e, b):
                sp.dma_start(d_in[:, b], w_down[bass.ds(e, 1)].rearrange("e (k p) d -> p (e k) d", p=P)
                             ).then_inc(d_loaded[b], 16)

            sp.dma_start(tbl[:, :], table_rows).then_inc(consts_loaded, 16)
            sp.dma_start(ident[:, :], consts["ident"]).then_inc(consts_loaded, 16)
            for b in range(2):
                load_gu(b, b)
                load_d(b, b)

            def visit(e, b, i):
                if exists(e, 2):
                    sp.wait_ge(gu_hi_done, e + 1)
                    sp.wait_ge(gu_lo_done, e + 1)
                    load_gu(e + 2, b)
                    sp.wait_ge(d_hi_done, e + 1)
                    sp.wait_ge(d_lo_done, e + 1)
                    load_d(e + 2, b)
                if exists(e, -1):
                    store(e, b, i)

            def store(e, b, i):
                sp.wait_ge(y_done, e)
                sp.dma_start(y_rows[bass.ds((e - 1) * CAP, CAP), :].rearrange("(h p) d -> p h d", p=P),
                             y[:, 1 - b]).then_inc(y_stored[1 - b], 16)

            each_expert(sp, visit)
            store(E, 0, E // 2)
            for b in range(2):
                sp.wait_ge(y_stored[b], 16 * E // 2)

        @block.gpsimd
        def _(pool):
            def gather(e, b):
                nc.gpsimd.tensor_copy(index[:, b], tokens_of[:, bass.ds(e * HALVES, HALVES)]).then_inc(index_done, 1)
                pool.wait_ge(index_done, e + 1)
                pool.sem_inc(gathers_begun, 1)
                for n in range(HALVES):
                    pool.indirect_dma_start(xg[:, b, n, :], None, xn_rows,
                                            bass.IndirectOffsetOnAxis(ap=index[:, b, n:n + 1], axis=0)
                                            ).then_inc(gathered[b], 16)

            def split_gu(e, b):
                pool.wait_ge(gu_hi_done, e + 1)
                nc.gpsimd.tensor_tensor(gu_lo[:, b], gu_in[:, b], f32(gu_hi[:, b]), ALU.subtract).then_inc(gu_lo_done, 1)

            pool.wait_ge(tokens_done, 1)
            gather(0, 0)
            gather(1, 1)
            split_gu(0, 0)

            def visit(e, b, i):
                if exists(e, 2):
                    pool.wait_ge(xt_ready, e + 1)
                    gather(e + 2, b)
                if exists(e, 1):
                    split_gu(e + 1, 1 - b)
            each_expert(pool, visit)

        @block.tensor
        def _(pe):
            def turn(e, b, i):
                pe.wait_ge(gathered[b], 32 * (i + 1))
                wait(pe, xt_lo_done, e)
                for k in range(KD):
                    for n in range(HALVES):
                        mm = nc.tensor.transpose(xt_ps[:, k, P * n:P * (n + 1)], xg[:, b, n, P * k:P * (k + 1)],
                                                 ident[:, :])
                mm.then_inc(xt_ready, 1)

            def gate_up(e, b):
                pe.wait_ge(xt_hi_done, e + 1)
                pe.wait_ge(xt_lo_done, e + 1)
                pe.wait_ge(gu_hi_done, e + 1)
                pe.wait_ge(gu_lo_done, e + 1)
                wait(pe, h_done, e - 1)
                for w, ready in enumerate((gate_ready, up_ready)):
                    for f in range(KF):
                        for q, (wa, xa) in enumerate(PRODUCTS):
                            for k in range(KD):
                                mm = nc.tensor.matmul(gu_ps[:, b, w, f, :],
                                                      (gu_hi, gu_lo)[wa][:, b, w, k, P * f:P * (f + 1)],
                                                      (xt_hi, xt_lo)[xa][:, b, k, :],
                                                      start=(q == 0 and k == 0), stop=(q == 2 and k == KD - 1))
                    mm.then_inc(ready, 1)

            def down(e, b):
                pe.wait_ge(h_lo_done, e + 1)
                pe.wait_ge(d_hi_done, e + 1)
                pe.wait_ge(d_lo_done, e + 1)
                wait(pe, y_done, e)
                for n in range(HALVES):
                    for q, (wa, xa) in enumerate(PRODUCTS):
                        for k in range(KF):
                            mm = nc.tensor.matmul(y_ps[:, n, :], (h_hi, h_lo)[xa][:, b, k, P * n:P * (n + 1)],
                                                  (d_hi, d_lo)[wa][:, b, k, :],
                                                  start=(q == 0 and k == 0), stop=(q == 2 and k == KF - 1))
                mm.then_inc(y_ready, 1)

            pe.wait_ge(consts_loaded, 32)
            pe.wait_ge(tbl_f_done, 1)
            nc.tensor.transpose(y_ps[:, 0, 0:P], tbl_f[:, :], ident[:, :]).then_inc(tbl_turned, 1)
            turn(0, 0, 0)

            def visit(e, b, i):
                if exists(e, 1):
                    turn(e + 1, 1 - b, i + b)
                gate_up(e, b)
                if exists(e, -1):
                    down(e - 1, 1 - b)
            pe.wait_ge(tokens_done, 1)
            each_expert(pe, visit)
            down(E - 1, 1)

        @block.scalar
        def _(act):
            def split_x(e, b):
                act.wait_ge(xt_ready, e + 1)
                wait(act, up_ready, e - 1)
                nc.scalar.activation(xt_hi[:, b], xt_ps[:, :, :], ACT.Copy).then_inc(xt_hi_done, 1)

            def split_gu(e, b, i):
                act.wait_ge(gu_loaded[b], 32 * (i + 1))
                wait(act, up_ready, e - 1)
                nc.scalar.activation(gu_hi[:, b], gu_in[:, b], ACT.Copy).then_inc(gu_hi_done, 1)

            def split_d(e, b, i):
                act.wait_ge(d_loaded[b], 16 * (i + 1))
                wait(act, y_ready, e - 1)
                nc.scalar.activation(d_hi[:, b], d_in[:, b], ACT.Copy).then_inc(d_hi_done, 1)

            split_gu(0, 0, 0)
            split_x(0, 0)

            def visit(e, b, i):
                if exists(e, 1):
                    split_x(e + 1, 1 - b)
                    split_gu(e + 1, 1 - b, i + b)
                act.wait_ge(gate_ready, e + 1)
                wait(act, h_done, e - 1)
                nc.scalar.activation(act_g[:, b], gu_ps[:, b, 0], ACT.Silu).then_inc(act_done, 1)
                split_d(e, b, i)
                act.wait_ge(h_done, e + 1)
                wait(act, y_ready, e - 1)
                nc.scalar.activation(h_hi[:, b], h[:, b], ACT.Copy).then_inc(h_hi_done, 1)
            each_expert(act, visit)

        @block.vector
        def _(dve):
            dve.wait_ge(consts_loaded, 32)
            nc.vector.tensor_copy(tbl_f[:, :], tbl[:, :]).then_inc(tbl_f_done, 1)
            dve.wait_ge(tbl_turned, 1)
            nc.vector.tensor_copy(tokens_of[:, :], y_ps[:, 0, 0:P]).then_inc(tokens_done, 1)

            def split_x(e, b):
                dve.wait_ge(xt_hi_done, e + 1)
                nc.vector.tensor_tensor(xt_lo[:, b], xt_ps[:, :, :], f32(xt_hi[:, b]), ALU.subtract).then_inc(xt_lo_done, 1)

            split_x(0, 0)

            def copy_y(e, b, i):
                dve.wait_ge(y_ready, e + 1)
                wait(dve, y_stored[b], 16 * i)
                nc.vector.tensor_copy(y[:, b], y_ps[:, :, :]).then_inc(y_done, 1)

            def visit(e, b, i):
                if exists(e, 1):
                    split_x(e + 1, 1 - b)
                dve.wait_ge(act_done, e + 1)
                dve.wait_ge(up_ready, e + 1)
                wait(dve, h_hi_done, e - 1)
                wait(dve, h_lo_done, e - 1)
                nc.vector.tensor_tensor(h[:, b], act_g[:, b], gu_ps[:, b, 1], ALU.mult).then_inc(h_done, 1)
                dve.wait_ge(d_hi_done, e + 1)
                nc.vector.tensor_tensor(d_lo[:, b], d_in[:, b], f32(d_hi[:, b]), ALU.subtract).then_inc(d_lo_done, 1)
                dve.wait_ge(h_hi_done, e + 1)
                nc.vector.tensor_tensor(h_lo[:, b], h[:, b], f32(h_hi[:, b]), ALU.subtract).then_inc(h_lo_done, 1)
                if exists(e, -1):
                    copy_y(e - 1, 1 - b, i - 1 + b)
            each_expert(dve, visit)
            copy_y(E - 1, 1, E // 2 - 1)

def combine_phase(nc, consts, x, attnT, Wo, bo, y_rows, row_of, top_w, x1, xnT, next_w, next_parts):
    assert NC == KD
    with ExitStack() as ctx:
        sb = lambda name, shape, dt: ctx.enter_context(nc.sbuf_tensor(f"comb_{name}", shape, dt))
        sem = ctx.enter_context(semaphores(nc, "comb"))
        w = sb("w", [P, NG, D], F32)
        w_parts = [sb("w_hi", [P, NG, D], F32R), sb("w_lo", [P, NG, D], F32R)]
        bias = sb("bias", [P, D], F32)
        ident = sb("ident", [P, P], F32)
        eps = sb("eps", [P, 1], F32)
        a_in = sb("a_in", [P, 2, NG, P], F32)
        a_parts = [sb("a_hi", [P, 2, NG, P], F32R), sb("a_lo", [P, 2, NG, P], F32R)]
        x_in = sb("x_in", [P, 2, D], F32)
        index = sb("index", [P, TPC, K], U32)
        weight = sb("weight", [P, TPC, K], F32)
        yg = sb("yg", [P, TPC, K, D], F32)
        total = sb("total", [P, 2, D], F32)
        scrap = sb("scrap", [P, D], F32)
        row_sum, less_mean, squares, std, rstd = (sb(n, [P, 2], F32) for n in (
            "row_sum", "less_mean", "squares", "std", "rstd"))
        xn = sb("xn", [P, 2, D], F32)
        xT = [sb("xT_hi", [P, KD, CH], F32R), sb("xT_lo", [P, KD, CH], F32R)]
        o_ps = ctx.enter_context(nc.psum_tensor("comb_o_ps", [P, 2, D], F32))
        xT_ps = ctx.enter_context(nc.psum_tensor("comb_xT_ps", [P, 2, KD, P], F32))
        consts_loaded, w_hi_done, w_lo_done = sem("consts_loaded"), sem("w_hi_done"), sem("w_lo_done")
        next_loaded, next_hi_done = sem("next_loaded"), sem("next_hi_done")
        in_loaded, stored = ([sem(f"{n}{b}") for b in range(2)] for n in ("in_loaded", "stored"))
        gathered = [sem(f"gathered{t}") for t in range(TPC)]
        parts_stored = [sem("hi_stored"), sem("lo_stored")]
        (a_hi_done, a_lo_done, o_ready, small_done, biased, summed, eps_set, row_summed, mean_done, squared, std_done,
         rstd_done, xn_done, turned, hi_done, lo_done) = (
            sem(n) for n in ("a_hi_done", "a_lo_done", "o_ready", "small_done", "biased", "summed", "eps_set",
                             "row_summed", "mean_done", "squared", "std_done", "rstd_done", "xn_done", "turned",
                             "hi_done", "lo_done"))
        SUMS = K + 1
        block = ctx.enter_context(nc.Block())

        def tiles(eng, visit):
            with eng.Fori(0, NC - 1) as c:
                for t in range(TPC):
                    visit(c, t, TPC * c + t, TPC)
            for t in range(TPC):
                visit(NC - 1, t, NT - TPC + t, TPC - 1 - t)

        @block.sync
        def _(sp):
            def load(n, b):
                sp.dma_start(a_in[:, b], attnT[:, :, bass.ds(n * P, P)].rearrange("g p t -> p g t")).then_inc(in_loaded[b], 16)
                sp.dma_start(x_in[:, b], x[bass.ds(n * P, P), :]).then_inc(in_loaded[b], 16)

            def visit(c, t, n, ahead):
                b = t % 2
                if t == 0:
                    sp.wait_ge(w_lo_done, c + 1)
                    sp.dma_start(w[:, :, :].rearrange("p g d -> p (g d)"), next_w[bass.ds(c * P, P), :]).then_inc(next_loaded, 16)
                sp.wait_ge(summed, (n + 1) * SUMS)
                sp.dma_start(x1[bass.ds(n * P, P), :], total[:, b]).then_inc(stored[b], 16)
                if ahead >= 2:
                    load(n + 2, b)
                if t == TPC - 1:
                    for part, done in ((HI, hi_done), (LO, lo_done)):
                        sp.wait_ge(done, n + 1 + 2 * part)
                        sp.dma_start(xnT[part][bass.ds(c, 1)].rearrange("c p k t -> (c p) k t"), f32(xT[part][:, :, :])
                                     ).then_inc(parts_stored[part], 16)

            sp.dma_start(w[:, :, :], Wo.rearrange("(g p) d -> p g d", p=P)).then_inc(consts_loaded, 16)
            sp.dma_start(bias[:, :], bo.unsqueeze(0).broadcast_to([P, D])).then_inc(consts_loaded, 16)
            sp.dma_start(ident[:, :], consts["ident"]).then_inc(consts_loaded, 16)
            for b in range(2):
                load(b, b)
            tiles(sp, visit)
            for b in range(2):
                sp.wait_ge(stored[b], 16 * (1 + NT // 2))
                sp.wait_ge(parts_stored[b], 16 * (1 + NC))

        @block.gpsimd
        def _(pool):
            def fetch(n, t):
                nc.gpsimd.tensor_copy(index[:, t], row_of[:, bass.ds(n, 1), :].rearrange("p a k -> p (a k)")
                                      ).then_inc(small_done, 1)
                pool.wait_ge(small_done, 2 * n + 1)
                nc.gpsimd.tensor_copy(weight[:, t], top_w[:, bass.ds(n, 1), :].rearrange("p a k -> p (a k)")
                                      ).then_inc(small_done, 1)
                for k in range(K):
                    pool.indirect_dma_start(yg[:, t, k, :], None, y_rows,
                                            bass.IndirectOffsetOnAxis(ap=index[:, t, k:k + 1], axis=0)
                                            ).then_inc(gathered[t], 16)

            def visit(c, t, n, ahead):
                if ahead == TPC:
                    pool.wait_ge(summed, (n + 1) * SUMS)
                    fetch(n + TPC, t)

            for t in range(TPC):
                fetch(t, t)
            tiles(pool, visit)

        @block.scalar
        def _(act):
            def high_a(c, t, n):
                act.wait_ge(in_loaded[t % 2], 32 * (2 * c + t // 2 + 1))
                act.wait_ge(o_ready, n + 1)
                nc.scalar.activation(a_parts[HI][:, t % 2], a_in[:, t % 2], ACT.Copy).then_inc(a_hi_done, 1)

            def visit(c, t, n, ahead):
                b = t % 2
                if ahead:
                    high_a(c + (t + 1) // TPC, (t + 1) % TPC, n + 1)
                act.wait_ge(summed, (n + 1) * SUMS)
                nc.scalar.activation(scrap[:, :], total[:, b], ACT.Copy, accum_out=row_sum[:, b:b + 1]).then_inc(row_summed, 1)
                act.wait_ge(row_summed, n + 1)
                act.wait_ge(mean_done, n + 1)
                nc.scalar.activation(scrap[:, :], total[:, b], ACT.Square, bias=less_mean[:, b:b + 1],
                                     accum_out=squares[:, b:b + 1]).then_inc(squared, 1)
                act.wait_ge(squared, n + 1)
                nc.scalar.activation(std[:, b:b + 1], squares[:, b:b + 1], ACT.Sqrt, bias=eps[:, 0:1],
                                     scale=1.0 / D).then_inc(std_done, 1)
                if t == 2:
                    act.wait_ge(next_loaded, 16 * (c + 1))
                    nc.scalar.activation(next_parts[HI][:, bass.ds(c, 1), :].rearrange("p a f -> p (a f)"),
                                         w[:, :, :].rearrange("p g d -> p (g d)"), ACT.Copy).then_inc(next_hi_done, 1)
                act.wait_ge(turned, n + 1)
                if t == 0:
                    act.wait_ge(parts_stored[HI], 16 * (c + 1))
                nc.scalar.activation(xT[HI][:, :, P * t:P * (t + 1)], xT_ps[:, b], ACT.Copy).then_inc(hi_done, 1)

            act.wait_ge(consts_loaded, 48)
            nc.scalar.activation(w_parts[HI][:, :, :], w[:, :, :], ACT.Copy).then_inc(w_hi_done, 1)
            for b in range(2):
                act.sem_inc(stored[b], 16)
                act.sem_inc(parts_stored[b], 16)
            act.sem_inc(o_ready, 2)
            act.wait_ge(eps_set, 1)
            high_a(0, 0, 0)
            tiles(act, visit)

        @block.tensor
        def _(pe):
            def project(n, b):
                pe.wait_ge(a_hi_done, n + 1)
                pe.wait_ge(a_lo_done, n + 1)
                pe.wait_ge(biased, n + 1)
                for q, (wa, xa) in enumerate(PRODUCTS):
                    for g in range(NG):
                        mm = nc.tensor.matmul(o_ps[:, b, :], a_parts[xa][:, b, g, :], w_parts[wa][:, g, :],
                                              start=(q == 0 and g == 0), stop=(q == 2 and g == NG - 1))
                mm.then_inc(o_ready, 1)

            def visit(c, t, n, ahead):
                b = t % 2
                if ahead:
                    project(n + 1, 1 - b)
                pe.wait_ge(xn_done, n + 1)
                pe.wait_ge(lo_done, n + 1)
                for k in range(KD):
                    mm = nc.tensor.transpose(xT_ps[:, b, k, :], xn[:, b, P * k:P * (k + 1)], ident[:, :])
                mm.then_inc(turned, 1)

            pe.wait_ge(w_hi_done, 1)
            pe.wait_ge(w_lo_done, 1)
            project(0, 0)
            tiles(pe, visit)

        @block.vector
        def _(dve):
            def low_a(n, b):
                dve.wait_ge(a_hi_done, n + 1)
                nc.vector.tensor_tensor(a_parts[LO][:, b], a_in[:, b], f32(a_parts[HI][:, b]), ALU.subtract).then_inc(a_lo_done, 1)

            def begin(c, t, n):
                b = t % 2
                dve.wait_ge(o_ready, n + 3)
                dve.wait_ge(stored[b], 16 * (2 * c + t // 2 + 1))
                nc.vector.tensor_tensor(total[:, b], o_ps[:, b, :], bias[:, :], ALU.add).then_inc(biased, 1)
                dve.wait_ge(biased, n + 3)
                nc.vector.tensor_tensor(total[:, b], total[:, b], x_in[:, b], ALU.add).then_inc(summed, 1)

            def visit(c, t, n, ahead):
                b = t % 2
                if ahead:
                    low_a(n + 1, 1 - b)
                dve.wait_ge(gathered[t], 16 * K * (c + 1))
                dve.wait_ge(small_done, 2 * n + 2)
                for k in range(K):
                    dve.wait_ge(summed, n * SUMS + k + 1)
                    nc.vector.scalar_tensor_tensor(total[:, b], yg[:, t, k, :], weight[:, t, k:k + 1], total[:, b],
                                                   ALU.mult, ALU.add).then_inc(summed, 1)
                dve.wait_ge(row_summed, n + 1)
                nc.vector.tensor_scalar(less_mean[:, b:b + 1], row_sum[:, b:b + 1], -1.0 / D, None,
                                        ALU.mult).then_inc(mean_done, 1)
                if ahead:
                    begin(c + (t + 1) // TPC, (t + 1) % TPC, n + 1)
                dve.wait_ge(std_done, n + 1)
                nc.vector.reciprocal(rstd[:, b:b + 1], std[:, b:b + 1]).then_inc(rstd_done, 1)
                dve.wait_ge(rstd_done, n + 1)
                nc.vector.tensor_scalar(xn[:, b], total[:, b], less_mean[:, b:b + 1], rstd[:, b:b + 1], ALU.add,
                                        ALU.mult).then_inc(xn_done, 1)
                dve.wait_ge(hi_done, n + 1)
                if t == 0:
                    dve.wait_ge(parts_stored[LO], 16 * (c + 1))
                here = (slice(None), slice(None), slice(P * t, P * (t + 1)))
                nc.vector.tensor_tensor(xT[LO][here], xT_ps[:, b], f32(xT[HI][here]), ALU.subtract).then_inc(lo_done, 1)
                if t == 2:
                    dve.wait_ge(next_hi_done, c + 1)
                    hi, lo = (next_parts[part][:, bass.ds(c, 1), :].rearrange("p a f -> p (a f)") for part in (HI, LO))
                    nc.vector.tensor_tensor(lo, w[:, :, :].rearrange("p g d -> p (g d)"), f32(hi),
                                            ALU.subtract).then_inc(w_lo_done, 1)

            nc.vector.memset(eps[:, :], LN_EPS).then_inc(eps_set, 1)
            dve.sem_inc(biased, 2)
            dve.sem_inc(lo_done, 2)
            dve.wait_ge(w_hi_done, 1)
            nc.vector.tensor_tensor(w_parts[LO][:, :, :], w[:, :, :], f32(w_parts[HI][:, :, :]),
                                    ALU.subtract).then_inc(w_lo_done, 1)
            low_a(0, 0)
            begin(0, 0, 0)
            tiles(dve, visit)

DI, DS, RANK = 1024, 16, 32
KI = DI // P
SSM = RANK + 2 * DS
TAPS = 4

def mamba_in_phase(nc, consts, xnT, in_parts, conv_w, conv_b, x_wT, dt_wT, dt_b, xt_d, sg_d, dt_d, u_d, bc_d):
    with ExitStack() as ctx:
        sb = lambda name, shape, dt: ctx.enter_context(nc.sbuf_tensor(f"min_{name}", shape, dt))
        ps = lambda name, shape, dt: ctx.enter_context(nc.psum_tensor(f"min_{name}", shape, dt))
        sem = ctx.enter_context(semaphores(nc, "min"))
        HALF = KI // 2
        scratch = sb("scratch", [P, 4, 4, CH], F32)
        z, ex, lw, fix = (scratch[:, n] for n in range(4))
        xw_in = sb("xw_in", [P, KI, SSM], F32)
        xw = [sb("xw_hi", [P, KI, SSM], F32R), sb("xw_lo", [P, KI, SSM], F32R)]
        dw = [sb("dw_hi", [RANK, DI], F32R), sb("dw_lo", [RANK, DI], F32R)]
        taps = sb("taps", [P, KI, TAPS], F32)
        cb, db = sb("cb", [P, KI], F32), sb("db", [P, KI], F32)
        xc = sb("xc", [P, 2, 2, KD, CH], F32R)
        halo = TAPS - 1
        raw = sb("raw", [P, KI, CH + halo + 1], F32)
        conv = sb("conv", [P, 2, CH], F32)
        xt = sb("xt", [P, KI, CH], F32)
        xt_parts = [sb("xt_hi", [P, 2, CH], F32R), sb("xt_lo", [P, 2, CH], F32R)]
        sg = sb("sg", [P, 2, CH], F32)
        ts = [sb("ts_hi", [RANK, CH], F32R), sb("ts_lo", [RANK, CH], F32R)]
        bc = sb("bc", [SSM, CH], F32)
        dw_in = scratch[0:RANK, 2, 0:2].rearrange("p a t -> p (a t)")
        dt = sb("dt", [P, HALF, CH], F32)
        u = fix
        one = sb("one", [P, 1], F32)
        acc = ps("acc", [P, 4, CH], F32)
        ssm_ps = ps("ssm_ps", [SSM, CH], F32)
        dt_ps = ps("dt_ps", [P, 2, CH], F32)

        consts_loaded = sem("consts_loaded")
        xc_loaded = [sem(f"xc_loaded{b}") for b in range(2)]
        xt_stored = [sem(f"xt_stored{m}") for m in range(KI)]
        sg_stored, du_stored = [sem(f"sg_stored{b}") for b in range(2)], [sem(f"du_stored{m}") for m in range(HALF)]
        bc_stored = sem("bc_stored")
        (small_hi_done, small_lo_done, one_set, acc_ready, acc_read, halo_done, conv_step,
         xt_done, xt_hi_done, xt_lo_done, xproj_done, bc_done, ts_hi_done, ts_lo_done, dt_ready, z_done, abs_done,
         ex_done, lw_done, fix_step, dt_done, u_done, wm_done, lw_masked, halo_set) = (sem(n) for n in (
             "small_hi_done", "small_lo_done", "one_set", "acc_ready", "acc_read",
             "halo_done", "conv_step", "xt_done", "xt_hi_done", "xt_lo_done", "xproj_done", "bc_done", "ts_hi_done",
             "ts_lo_done", "dt_ready", "z_done", "abs_done", "ex_done", "lw_done", "fix_step", "dt_done", "u_done", "wm_done", "lw_masked", "halo_set"))
        MT = 2 * KI
        SILU_LAG, XPROJ_LAG = 2, 4
        DT_AT = KI + XPROJ_LAG + 2
        block = ctx.enter_context(nc.Block())

        def chunks(eng):
            with eng.Fori(0, NC // 2) as i:
                for b in range(2):
                    yield i, b, 2 * i + b

        @block.sync
        def _(sp):
            def load(chunk, b):
                for part in (HI, LO):
                    sp.dma_start(f32(xc[:, b, part]), xnT[part][chunk]).then_inc(xc_loaded[b], 16)

            for b in range(2):
                load(b, b)

            def store_dt(n, first):
                for m in range(first, first + HALF):
                    sp.wait_ge(dt_done, n * KI + m + 5)
                    sp.dma_start(dt_d[bass.ds(n, 1), :, m, :].rearrange("c p t -> (c p) t"), dt[:, m % HALF]).then_inc(du_stored[m % HALF], 16)
                    sp.wait_ge(u_done, n * KI + m + 1 + KI)
                    sp.dma_start(u_d[bass.ds(n, 1), :, m, :].rearrange("c p t -> (c p) t"), u[:, m % HALF]).then_inc(du_stored[m % HALF], 16)

            def chunk(n, b, more):
                for m in range(KI):
                    sp.wait_ge(xt_done, n * KI + m + 2)
                    sp.dma_start(xt_d[bass.ds(n, 1), :, m, :].rearrange("c p t -> (c p) t"), xt[:, m]).then_inc(xt_stored[m], 16)
                for m in range(KI):
                    sp.wait_ge(acc_read, n * MT + KI + m + 5)
                    sp.dma_start(sg_d[bass.ds(n, 1), :, m, :].rearrange("c p t -> (c p) t"), sg[:, m % 2]).then_inc(sg_stored[m % 2], 16)
                if more:
                    load(n + 2, b)
                sp.wait_ge(bc_done, n + 2)
                sp.dma_start(bc_d[:, bass.ds(n * CH, CH)], bc[RANK:SSM, :]).then_inc(bc_stored, 16)
                store_dt(n, 0)
                store_dt(n, HALF)

            with sp.Fori(0, NC // 2 - 1) as i:
                for b in range(2):
                    chunk(2 * i + b, b, True)
            for b in range(2):
                chunk(NC - 2 + b, b, False)
            for m in range(KI):
                sp.wait_ge(xt_stored[m], 16 * (1 + NC))
            for b in range(2):
                sp.wait_ge(sg_stored[b], 16 * (1 + NC * KI // 2))
            for m in range(HALF):
                sp.wait_ge(du_stored[m], 32 * (1 + 2 * NC))
            sp.wait_ge(bc_stored, 16 * (1 + NC))

        @block.tensor
        def _(pe):
            def x_proj(n, m):
                pe.wait_ge(xt_hi_done, n * KI + m + 1)
                pe.wait_ge(xt_lo_done, n * KI + m + 1)
                if m == 0:
                    pe.wait_ge(ts_lo_done, n + 1)
                    pe.wait_ge(bc_done, n + 1)
                for q, (wa, xa) in enumerate(PRODUCTS):
                    mm = nc.tensor.matmul(ssm_ps[:, :], xw[wa][:, m, :], xt_parts[xa][:, m % 2],
                                          start=(m == 0 and q == 0), stop=(m == KI - 1 and q == 2))
                mm.then_inc(xproj_done, 1)

            def dt_proj(n, m):
                pe.wait_ge(ts_hi_done, n + 1)
                pe.wait_ge(ts_lo_done, n + 2)
                pe.wait_ge(z_done, n * KI + m + 1)
                for q, (wa, xa) in enumerate(PRODUCTS):
                    mm = nc.tensor.matmul(dt_ps[:, m % 2, :], dw[wa][:, P * m:P * (m + 1)], ts[xa][:, :],
                                          start=(q == 0), stop=(q == 2))
                mm.then_inc(dt_ready, 1)

            pe.wait_ge(small_hi_done, 2)
            pe.wait_ge(small_lo_done, 2)
            for i, b, n in chunks(pe):
                pe.wait_ge(xc_loaded[b], 32 * (i + 1))
                for m in range(MT):
                    if m in (DT_AT, DT_AT + 1):
                        dt_proj(n, 2 * (m - DT_AT))
                        dt_proj(n, 2 * (m - DT_AT) + 1)
                    pe.wait_ge(acc_read, n * MT + m + 1)
                    for q, (wa, xa) in enumerate(PRODUCTS):
                        for k in range(KD):
                            mm = nc.tensor.matmul(acc[:, m % 4], in_parts[wa][:, k, P * m:P * (m + 1)],
                                                  xc[:, b, xa, k, :], start=(q == 0 and k == 0),
                                                  stop=(q == 2 and k == KD - 1))
                    mm.then_inc(acc_ready, 1)
                    if XPROJ_LAG <= m < XPROJ_LAG + KI:
                        x_proj(n, m - XPROJ_LAG)
                for m in range(HALF, KI):
                    dt_proj(n, m)

        @block.scalar
        def _(act):
            act.dma_start(xw_in[:, :, :], x_wT.rearrange("(k p) s -> p k s", p=P)).then_inc(consts_loaded, 16)
            act.dma_start(dw_in[:, :], dt_wT).then_inc(consts_loaded, 16)
            act.dma_start(taps[:, :, :], conv_w.rearrange("(m p) j -> p m j", p=P)).then_inc(consts_loaded, 16)
            act.dma_start(cb[:, :], conv_b).then_inc(consts_loaded, 16)
            act.dma_start(db[:, :], dt_b).then_inc(consts_loaded, 16)
            for m in range(KI):
                act.sem_inc(xt_stored[m], 16)
            for b in range(2):
                act.sem_inc(sg_stored[b], 16)
            for m in range(HALF):
                act.sem_inc(du_stored[m], 32)
            act.sem_inc(bc_stored, 16)
            act.wait_ge(consts_loaded, 80)
            nc.scalar.activation(xw[HI][:, :, :], xw_in[:, :, :], ACT.Copy).then_inc(small_hi_done, 1)
            nc.scalar.activation(dw[HI][:, :], dw_in[:, :], ACT.Copy).then_inc(small_hi_done, 1)
            act.wait_ge(one_set, 1)

            def silu_x(n, m):
                act.wait_ge(conv_step, (n * KI + m + 1) * TAPS)
                act.wait_ge(xt_stored[m], 16 * (n + 1))
                act.wait_ge(u_done, n * KI + m + 1)
                nc.scalar.activation(xt[:, m], conv[:, m % 2], ACT.Silu, bias=cb[:, m:m + 1]).then_inc(xt_done, 1)
                act.wait_ge(xt_done, n * KI + m + 2)
                if m >= 2:
                    act.wait_ge(xproj_done, n * KI + m - 1)
                nc.scalar.activation(xt_parts[HI][:, m % 2], xt[:, m], ACT.Copy).then_inc(xt_hi_done, 1)

            def softplus(n, first):
                for m in range(first, first + HALF):
                    s = n * KI + m
                    act.wait_ge(dt_ready, s + 1)
                    act.wait_ge(dt_done, s + 1)
                    nc.scalar.activation(z[:, m % 4], dt_ps[:, m % 2], ACT.Identity, bias=db[:, m:m + 1]).then_inc(z_done, 1)
                    act.wait_ge(z_done, s + 3)
                    nc.scalar.activation(ex[:, m % 4], z[:, m % 4], ACT.Abs).then_inc(abs_done, 1)
                    act.wait_ge(abs_done, s + 1)
                    nc.scalar.activation(ex[:, m % 4], ex[:, m % 4], ACT.Exp, scale=-1.0).then_inc(ex_done, 1)
                for m in range(first, first + HALF):
                    act.wait_ge(ex_done, n * KI + m + 1)
                    nc.scalar.activation(lw[:, m % 4], ex[:, m % 4], ACT.Ln, bias=one[:, 0:1]).then_inc(lw_done, 1)

            for i, b, n in chunks(act):
                for m in range(MT):
                    if m < MT:
                        act.wait_ge(acc_ready, n * MT + m + 1)
                        if m < KI:
                            act.wait_ge(halo_done, (n + 1) * KI + m + 1 - KI)
                            nc.scalar.activation(raw[:, m, halo:halo + CH], acc[:, m % 4], ACT.Copy).then_inc(acc_read, 1)
                        else:
                            act.wait_ge(sg_stored[m % 2], 16 * (n * KI // 2 + (m - KI) // 2 + 1))
                            nc.scalar.activation(sg[:, m % 2], acc[:, m % 4], ACT.Silu).then_inc(acc_read, 1)
                    if SILU_LAG <= m < SILU_LAG + KI:
                        silu_x(n, m - SILU_LAG)
                    if m == KI + XPROJ_LAG:
                        act.wait_ge(xproj_done, (n + 1) * KI)
                        nc.scalar.activation(ts[HI][:, :], ssm_ps[0:RANK, :], ACT.Copy).then_inc(ts_hi_done, 1)
                        act.wait_ge(bc_stored, 16 * (n + 1))
                        nc.scalar.activation(bc[RANK:SSM, :], ssm_ps[RANK:SSM, :], ACT.Copy).then_inc(bc_done, 1)
                    if m == DT_AT - 1:
                        softplus(n, 0)
                softplus(n, HALF)

        @block.gpsimd
        def _(pool):
            pool.sem_inc(ts_lo_done, 1)
            pool.sem_inc(dt_done, 4)
            pool.sem_inc(z_done, 2)
            pool.sem_inc(acc_read, 4)
            for sem_ in (xt_done, bc_done):
                pool.sem_inc(sem_, 1)
            pool.sem_inc(u_done, KI)
            for i, b, n in chunks(pool):
                for m in range(KI):
                    s = n * KI + m
                    pool.wait_ge(lw_masked, s * 2 + 2)
                    nc.gpsimd.tensor_tensor(fix[:, m % 4], lw[:, m % 4], fix[:, m % 4], ALU.add).then_inc(fix_step, 1)
                    pool.wait_ge(dt_done, s + 5)
                    nc.gpsimd.tensor_tensor(u[:, m % HALF], dt[:, m % HALF], xt[:, m], ALU.mult).then_inc(u_done, 1)

        @block.vector
        def _(dve):
            nc.vector.memset(one[:, :], 1.0).then_inc(one_set, 1)
            nc.vector.memset(raw[:, :, 0:halo], 0.0).then_inc(halo_set, 1)
            dve.wait_ge(halo_set, 1)
            dve.sem_inc(halo_done, KI)
            dve.wait_ge(small_hi_done, 2)
            nc.vector.tensor_tensor(xw[LO][:, :, :], xw_in[:, :, :], f32(xw[HI][:, :, :]), ALU.subtract).then_inc(small_lo_done, 1)
            nc.vector.tensor_tensor(dw[LO][:, :], dw_in[:, :], f32(dw[HI][:, :]), ALU.subtract).then_inc(small_lo_done, 1)

            def convolve(n, b, m):
                dve.wait_ge(acc_read, n * MT + m + 5)
                dve.wait_ge(xt_done, n * KI + max(m, 1))
                c = (n * KI + m) * TAPS
                nc.vector.tensor_scalar(conv[:, m % 2], raw[:, m, 0:CH], taps[:, m, 0:1], None, ALU.mult).then_inc(conv_step, 1)
                for j in range(1, TAPS):
                    dve.wait_ge(conv_step, c + j)
                    nc.vector.scalar_tensor_tensor(conv[:, m % 2], raw[:, m, j:j + CH], taps[:, m, j:j + 1],
                                                   conv[:, m % 2], ALU.mult, ALU.add).then_inc(conv_step, 1)
                dve.wait_ge(conv_step, c + TAPS)
                if b == 0:
                    nc.vector.tensor_copy(raw[:, m, 0:halo], raw[:, m, CH:CH + halo]).then_inc(halo_done, 1)
                else:
                    nc.vector.memset(raw[:, m, 0:halo], 0.0).then_inc(halo_done, 1)

            def low_x(n, m):
                dve.wait_ge(xt_hi_done, n * KI + m + 1)
                nc.vector.tensor_tensor(xt_parts[LO][:, m % 2], xt[:, m], f32(xt_parts[HI][:, m % 2]),
                                        ALU.subtract).then_inc(xt_lo_done, 1)

            def softplus(n, first):
                for m in range(first, first + HALF):
                    s = n * KI + m
                    dve.wait_ge(ex_done, s + 1)
                    dve.wait_ge(du_stored[m % HALF], 32 * (n * 2 + m // HALF + 1))
                    nc.vector.tensor_scalar(fix[:, m % 4], ex[:, m % 4], 1.0, 1.0, ALU.add, ALU.subtract).then_inc(wm_done, 1)
                for m in range(first, first + HALF + 1):
                    s = n * KI + m
                    if m < first + HALF:
                        dve.wait_ge(wm_done, s + 1)
                        dve.wait_ge(lw_done, s + 1)
                        nc.vector.scalar_tensor_tensor(lw[:, m % 4], fix[:, m % 4], 0.0, lw[:, m % 4],
                                                       ALU.is_gt, ALU.mult).then_inc(lw_masked, 1)
                        dve.wait_ge(lw_masked, s * 2 + 1)
                        nc.vector.tensor_tensor(fix[:, m % 4], ex[:, m % 4], fix[:, m % 4], ALU.subtract).then_inc(lw_masked, 1)
                    if m > first:
                        r = m - 1
                        dve.wait_ge(fix_step, n * KI + r + 1)
                        dve.wait_ge(u_done, n * KI + r + 1 - HALF + KI)
                        nc.vector.scalar_tensor_tensor(dt[:, r % HALF], z[:, r % 4], 0.0, fix[:, r % 4],
                                                       ALU.max, ALU.add).then_inc(dt_done, 1)

            for i, b, n in chunks(dve):
                for m in range(KI + 1):
                    if m < KI:
                        convolve(n, b, m)
                    if m >= 1:
                        low_x(n, m - 1)
                dve.wait_ge(ts_hi_done, n + 1)
                nc.vector.tensor_tensor(ts[LO][:, :], ssm_ps[0:RANK, :], f32(ts[HI][:, :]), ALU.subtract).then_inc(ts_lo_done, 1)
                softplus(n, 0)
                softplus(n, HALF)

def scan_ffn_phase(nc, consts, xnT, x1, tern_d, scales, A, Dp, out_wT, xt_d, sg_d, dt_d, u_d, bc_d, result):
    SPS, CPS = 4, P // 4
    SG, CG = DS // SPS, P // CPS
    TILE = SG * CG
    STEPS = KI * TILE
    PER_F = STEPS // FT
    MM = 24
    assert MM == 3 * PER_F
    NBUF = 4
    OUTS = 2 * CG
    with ExitStack() as ctx:
        sb = lambda name, shape, dt: ctx.enter_context(nc.sbuf_tensor(f"scan_{name}", shape, dt))
        ps = lambda name, shape, dt: ctx.enter_context(nc.psum_tensor(f"scan_{name}", shape, dt))
        sem = ctx.enter_context(semaphores(nc, "scan"))
        bc = sb("bc", [P, SG, 2, CH], F32)
        dtb, ub = (sb(n, [P, 2, CG, CH], F32) for n in ("dtb", "ub"))
        xtb, sgb = (sb(n, [P, 2, CH], F32) for n in ("xtb", "sgb"))
        decay, inp, state = (sb(n, [P, NBUF, CH], F32) for n in ("decay", "inp", "state"))
        out = sb("out", [P, OUTS, CH], F32)
        carry = sb("carry", [P, STEPS], F32)
        a_sb, d_sb = sb("a", [P, KI * CG, SG], F32), sb("d", [P, KI], F32)
        ident = sb("ident", [P, P], F32)
        sel = sb("sel", [P, CPS], F32)
        dmat = sb("dmat", [P, KI, P], F32)
        out_w = sb("out_w", [P, KI, D], F32)
        yg = sb("yg", [P, 2, CH], F32)
        tern = sb("tern", [P, 4, 3, CH], F32R)
        xc = sb("xc", [P, 2, 2, KD, CH], F32R)
        x_io = sb("x_io", [P, TPC, D], F32)
        th, up, h = (sb(n, [P, 2, CH], F32) for n in ("th", "up", "h"))
        h_parts = [sb("h_hi", [P, 2, CH], F32R), sb("h_lo", [P, 2, CH], F32R)]
        y_ps = ps("y_ps", [P, 2, CH], F32)
        ug_ps = ps("ug_ps", [P, 2, CH], F32)
        f_ps = ps("f_ps", [P, TPC, D], F32)

        consts_loaded, tables_done = sem("consts_loaded"), sem("tables_done")
        bc_loaded = [sem(f"bc_loaded{s}") for s in range(SG)]
        du_loaded, xs_loaded, xc_loaded = ([sem(f"{n}{b}") for b in range(2)] for n in (
            "du_loaded", "xs_loaded", "xc_loaded"))
        tern_loaded = [sem(f"tern_loaded{b}") for b in range(4)]
        x_loaded, x_stored, w_loaded = sem("x_loaded"), sem("x_stored"), sem("w_loaded")
        (decay_done, inp_done, scan_done, carried, out_done, out_used, yg_done, projected, u_ready, g_ready, th_done,
         up_done, h_done, h_hi_done, h_lo_done, d_ready, x_done) = (sem(n) for n in (
             "decay_done", "inp_done", "scan_done", "carried", "out_done", "out_used", "yg_done", "projected", "u_ready",
             "g_ready", "th_done", "up_done", "h_done", "h_hi_done", "h_lo_done", "d_ready", "x_done"))
        block = ctx.enter_context(nc.Block())

        def chunks(eng):
            with eng.Fori(0, NC // 2) as i:
                for b in range(2):
                    yield i, b, 2 * i + b

        @block.sync
        def _(sp):
            def load_states(n, g):
                for w in range(2):
                    row = w * DS + SPS * g
                    sp.dma_start(bc[:, g, w, :], bc_d[row:row + SPS, bass.ds(n * CH, CH)].unsqueeze(1).broadcast_to(
                        [SPS, CPS, CH])).then_inc(bc_loaded[g], 16)

            def load_du(n, d):
                for dst, src in ((dtb, dt_d), (ub, u_d)):
                    for s in range(SPS):
                        sp.dma_start(dst[CPS * s:CPS * (s + 1), d % 2], src[bass.ds(n, 1), :, d, :].rearrange(
                            "n (g c) t -> c (n g) t", c=CPS)).then_inc(du_loaded[d % 2], 16)

            def load_xs(n, d):
                for dst, src in ((xtb, xt_d), (sgb, sg_d)):
                    sp.dma_start(dst[:, d % 2], src[bass.ds(n, 1), :, d, :].rearrange("c p t -> (c p) t")
                                 ).then_inc(xs_loaded[d % 2], 16)

            def load_tern(f):
                sp.dma_start(f32(tern[:, f % 4]), tern_d[f]).then_inc(tern_loaded[f % 4], 16)

            def load_xc(n, b):
                for part in (HI, LO):
                    sp.dma_start(f32(xc[:, b, part]), xnT[part][bass.ds(n, 1)].rearrange("c p k t -> (c p) k t")
                                 ).then_inc(xc_loaded[b], 16)

            def store_x(n):
                sp.wait_ge(x_done, (n + 1) * TPC + 1)
                sp.dma_start(result[bass.ds(n * CH, CH), :].rearrange("(t p) d -> p t d", p=P), x_io[:, :, :]).then_inc(x_stored, 16)

            def chunk(n, b, more):
                for q in range(STEPS):
                    d, s = divmod(q, TILE)
                    f, r = divmod(q, PER_F)
                    if s == 1 and (d < KI - 1 or more):
                        sp.wait_ge(decay_done, n * STEPS + q)
                        sp.wait_ge(inp_done, n * STEPS + q)
                        load_du(*((n, d + 1) if d < KI - 1 else (n + 1, 0)))
                    if s == 5:
                        if d < KI - 1 or more:
                            if d or b:
                                sp.wait_ge(yg_done, n * KI + d + 2)
                            load_xs(*((n, d + 1) if d < KI - 1 else (n + 1, 0)))
                    if r == PER_F - 1 and (f < FT - 3 or more):
                        sp.wait_ge(d_ready, n * FT + f + 2)
                        load_tern((f + 3) % FT)
                    if q == 15 and b:
                        store_x(n - 1)
                    if q == 30:
                        sp.wait_ge(x_stored, 16 * (n + 1))
                        sp.dma_start(x_io[:, :, :], x1[bass.ds(n * CH, CH), :].rearrange("(t p) d -> p t d", p=P)
                                     ).then_inc(x_loaded, 16)
                        if more:
                            load_xc(n + 1, 1 - b)
                    if d == KI - 1 and more and s % CG == 1 and s > CG:
                        sp.wait_ge(out_done, n * STEPS + q - 1)
                        load_states(n + 1, s // CG - 1)
                if more:
                    sp.wait_ge(out_done, (n + 1) * STEPS)
                    load_states(n + 1, SG - 1)
                if b:
                    store_x(n)

            load_du(0, 0)
            load_states(0, 0)
            load_xc(0, 0)
            load_tern(0)
            for g in range(1, SG):
                load_states(0, g)
            load_xs(0, 0)
            for f in (1, 2):
                load_tern(f)
            with sp.Fori(0, NC // 2 - 1) as i:
                for b in range(2):
                    chunk(2 * i + b, b, True)
            for b in range(2):
                chunk(NC - 2 + b, b, b == 0)
            sp.wait_ge(x_stored, 16 * (1 + NC))

        @block.scalar
        def _(act):
            act.dma_start(a_sb[:, :, :], A).then_inc(consts_loaded, 16)
            act.dma_start(d_sb[:, :], Dp).then_inc(consts_loaded, 16)
            act.dma_start(ident[:, :], consts["ident"]).then_inc(consts_loaded, 16)
            act.dma_start(out_w[:, :, :], out_wT.rearrange("(m p) d -> p m d", p=P)).then_inc(w_loaded, 16)
            act.sem_inc(x_stored, 16)
            act.wait_ge(consts_loaded, 48)

            def carry_out(n, q):
                act.wait_ge(scan_done, n * STEPS + q + NBUF + 1)
                nc.scalar.activation(carry[:, q:q + 1], state[:, q % NBUF, CH - 1:CH], ACT.Copy).then_inc(carried, 1)

            for i, b, n in chunks(act):
                for q in range(STEPS):
                    d, s = divmod(q, TILE)
                    g, j = divmod(s, CG)
                    f, r = divmod(q, PER_F)
                    if s == 0:
                        act.wait_ge(du_loaded[d % 2], 128 * (n * KI // 2 + d // 2 + 1))
                    act.wait_ge(scan_done, n * STEPS + q + 1)
                    nc.scalar.activation(decay[:, q % NBUF], dtb[:, d % 2, j], ACT.Exp,
                                         scale=a_sb[:, CG * d + j, g:g + 1]).then_inc(decay_done, 1)
                    if b == 0 and q >= 2:
                        carry_out(n, q - 2)
                    if r == 4:
                        act.wait_ge(u_ready, n * FT + f + 1)
                        act.wait_ge(up_done, n * FT + f + 1)
                        nc.scalar.activation(th[:, f % 2], ug_ps[:, 0], ACT.Tanh, scale=scales[:, HALF_UP:HALF_UP + 1]).then_inc(th_done, 1)
                    if r == 7:
                        act.wait_ge(h_done, n * FT + f + 2)
                        act.wait_ge(d_ready, n * FT + f + 1)
                        nc.scalar.activation(h_parts[HI][:, f % 2], h[:, f % 2], ACT.Copy).then_inc(h_hi_done, 1)
                if b == 0:
                    for q in (STEPS - 2, STEPS - 1):
                        carry_out(n, q)

        @block.gpsimd
        def _(pool):
            pool.sem_inc(scan_done, NBUF)
            pool.sem_inc(out_used, OUTS)
            pool.sem_inc(up_done, 2)
            pool.sem_inc(d_ready, 2)
            pool.sem_inc(yg_done, 2)
            pool.sem_inc(projected, 2)
            for sem_ in (h_done, x_done, carried):
                pool.sem_inc(sem_, 1)

            def low_h(n, f):
                pool.wait_ge(h_hi_done, n * FT + f + 1)
                nc.gpsimd.tensor_tensor(h_parts[LO][:, f % 2], h[:, f % 2], f32(h_parts[HI][:, f % 2]),
                                        ALU.subtract).then_inc(h_lo_done, 1)

            for i, b, n in chunks(pool):
                for q in range(STEPS):
                    d, s = divmod(q, TILE)
                    g, j = divmod(s, CG)
                    f, r = divmod(q, PER_F)
                    if s == 0:
                        pool.wait_ge(du_loaded[d % 2], 128 * (n * KI // 2 + d // 2 + 1))
                    if d == 0 and j == 0:
                        pool.wait_ge(bc_loaded[g], 32 * (n + 1))
                    pool.wait_ge(scan_done, n * STEPS + q + 1)
                    nc.gpsimd.tensor_tensor(inp[:, q % NBUF], ub[:, d % 2, j], bc[:, g, 0, :], ALU.mult).then_inc(inp_done, 1)
                    if r == 1 and f:
                        low_h(n, f - 1)
                low_h(n, FT - 1)

        @block.tensor
        def _(pe):
            def ffn(n, b, m):
                f, r = divmod(m, MM)
                if r < 16:
                    which, kk = divmod(r, 8)
                    k, part = divmod(kk, 2)
                    if r == 0:
                        pe.wait_ge(tern_loaded[f % 4], 16 * (n * FT // 4 + f // 4 + 1))
                        pe.wait_ge(up_done, n * FT + f + 2)
                    if r == 8:
                        pe.wait_ge(h_done, n * FT + f + 1)
                    mm = nc.tensor.matmul(ug_ps[:, which, :], tern[:, f % 4, which, P * k:P * (k + 1)],
                                          xc[:, b, part, k, :], start=(kk == 0), stop=(kk == 7))
                    if kk == 7:
                        mm.then_inc((u_ready, g_ready)[which], 1)
                elif f:
                    down(n, f - 1, r - 16)

            def down(n, f, j):
                t, part = divmod(j, 2)
                if j == 0:
                    pe.wait_ge(h_lo_done, n * FT + f + 1)
                    if f == 0:
                        pe.wait_ge(x_done, n * TPC + 1)
                mm = nc.tensor.matmul(f_ps[:, t, :], h_parts[part][:, f % 2, P * t:P * (t + 1)],
                                      tern[:, f % 4, 2, :], start=(f == 0 and part == 0),
                                      stop=False)
                if j == 7:
                    mm.then_inc(d_ready, 1)

            def sum_states(n, batch):
                d, g = divmod(batch, SG)
                if g == 0:
                    pe.wait_ge(xs_loaded[d % 2], 32 * (n * KI // 2 + d // 2 + 1))
                    pe.wait_ge(yg_done, n * KI + d + 1)
                    nc.tensor.matmul(y_ps[:, d % 2, :], dmat[:, d, :], xtb[:, d % 2, :], start=True, stop=False)
                pe.wait_ge(out_done, n * STEPS + CG * (batch + 1))
                for j in range(CG):
                    nc.tensor.matmul(y_ps[CPS * j:CPS * (j + 1), d % 2, :], sel[:, :], out[:, (CG * batch + j) % OUTS, :],
                                     start=False, stop=(g == SG - 1)).then_inc(out_used, 1)

            def project(n, d):
                pe.wait_ge(yg_done, n * KI + d + 3)
                for t in range(TPC):
                    mm = nc.tensor.matmul(f_ps[:, t, :], yg[:, d % 2, P * t:P * (t + 1)], out_w[:, d % KI, :],
                                          start=False, stop=(d % KI == KI - 1))
                mm.then_inc(projected, 1)

            pe.wait_ge(tables_done, 1 + KI)
            pe.wait_ge(w_loaded, 16)
            for i, b, n in chunks(pe):
                pe.wait_ge(xc_loaded[b], 32 * (i + 1))
                for q in range(STEPS):
                    for m in range(3 * q, 3 * q + 3):
                        ffn(n, b, m)
                    if q and q % CG == 0:
                        sum_states(n, q // CG - 1)
                    if q % TILE == 6 and (q > TILE or b):
                        project(n, q // TILE - 1)
                sum_states(n, STEPS // CG - 1)
                for j in range(8):
                    down(n, FT - 1, j)
                if b:
                    project(n, KI - 1)

        @block.vector
        def _(dve):
            dve.wait_ge(consts_loaded, 48)
            nc.vector.tensor_reduce(sel[:, :], ident[:, :].rearrange("p (s c) -> p c s", c=CPS), AX_X,
                                    ALU.add).then_inc(tables_done, 1)
            for d in range(KI):
                nc.vector.tensor_scalar(dmat[:, d, :], ident[:, :], d_sb[:, d:d + 1], None, ALU.mult).then_inc(tables_done, 1)

            def times_c(n, q):
                d, s = divmod(q, TILE)
                if d == 0 and s % CG == 0:
                    dve.wait_ge(bc_loaded[s // CG], 32 * (n + 1))
                dve.wait_ge(scan_done, n * STEPS + q + NBUF + 1)
                dve.wait_ge(out_used, n * STEPS + q + 1)
                nc.vector.tensor_tensor(out[:, q % OUTS], state[:, q % NBUF], bc[:, s // CG, 1, :], ALU.mult).then_inc(out_done, 1)

            def gate_y(n, d):
                dve.wait_ge(out_used, n * STEPS + (d + 1) * TILE + OUTS)
                dve.wait_ge(xs_loaded[d % 2], 32 * (n * KI // 2 + (d + 2) // 2))
                dve.wait_ge(projected, n * KI + d + 1)
                nc.vector.tensor_tensor(yg[:, d % 2], y_ps[:, d % 2], sgb[:, d % 2], ALU.mult).then_inc(yg_done, 1)

            def add_ffn(n, t):
                dve.wait_ge(projected, (n + 1) * KI + 2)
                dve.wait_ge(x_loaded, 16 * (n + 1))
                nc.vector.tensor_tensor(x_io[:, t], f_ps[:, t, :], x_io[:, t], ALU.add).then_inc(x_done, 1)

            for i, b, n in chunks(dve):
                for q in range(STEPS):
                    d, s = divmod(q, TILE)
                    f, r = divmod(q, PER_F)
                    dve.wait_ge(decay_done, n * STEPS + q + 1)
                    dve.wait_ge(inp_done, n * STEPS + q + 1)
                    if b == 0:
                        dve.wait_ge(carried, i * STEPS + max(q - NBUF + 2, 1))
                    elif q == 0:
                        dve.wait_ge(carried, (i + 1) * STEPS + 1)
                    nc.vector.tensor_tensor_scan(state[:, q % NBUF], decay[:, q % NBUF], inp[:, q % NBUF],
                                                 0.0 if b == 0 else carry[:, q:q + 1], ALU.mult,
                                                 ALU.add).then_inc(scan_done, 1)
                    if q:
                        times_c(n, q - 1)
                    if r == 5:
                        dve.wait_ge(th_done, n * FT + f + 1)
                        nc.vector.scalar_tensor_tensor(up[:, f % 2], th[:, f % 2], 1.0, ug_ps[:, 0], ALU.add,
                                                       ALU.mult).then_inc(up_done, 1)
                    if r == 6:
                        dve.wait_ge(g_ready, n * FT + f + 1)
                        dve.wait_ge(up_done, n * FT + f + 3)
                        nc.vector.scalar_tensor_tensor(h[:, f % 2], ug_ps[:, 1], scales[:, PRODUCT:PRODUCT + 1], up[:, f % 2],
                                                       ALU.mult, ALU.mult).then_inc(h_done, 1)
                    if s == 3 and (d or b):
                        gate_y(n, d - 1)
                    if b and 9 <= q < 9 + TPC:
                        add_ffn(n - 1, q - 9)
                times_c(n, STEPS - 1)
                if b:
                    gate_y(n, KI - 1)
                    for t in range(TPC):
                        add_ffn(n, t)

def mega_layer_kernel(nc, ins, consts, result):
    def internal(name, shape, dt):
        return nc.dram_tensor(name, shape, dt, kind="Internal").ap()

    xn_rows = internal("xn_rows", [T + 1, D], F32)
    xnT = [[internal(f"xnT{layer}_{part}", [NC, P, KD, CH], F32) for part in ("hi", "lo")] for layer in range(2)]
    table = internal("table", [2 * NS, 1], I32)
    table_rows = table[0:NS, :].rearrange("(p c) a -> p (c a)", p=P)
    qk_parts = internal("qk_parts", [2, NG, 2, P, T], F32)
    v_rows = internal("v_rows", [T, D], F32)
    attnT = internal("attnT", [NG, P, T], F32)
    y_rows = internal("y_rows", [NS, D], F32)
    x1 = internal("x1", [T, D], F32)
    tern = internal("tern", [FT, P, 3, CH], F32)
    xt, sg, dt, u = (internal(n, [NC, P, KI, CH], F32) for n in ("m_xt", "m_sg", "m_dt", "m_u"))
    bc = internal("m_bc", [2 * DS, T], F32)

    ffn_wT = [ins[name] for name in ("W_upT", "W_gateT", "W_downT")]

    with ExitStack() as outer:
        scales = outer.enter_context(nc.sbuf_tensor("scales", [P, SCALES], F32))
        with ExitStack() as ctx:
            slot_of = ctx.enter_context(nc.sbuf_tensor("slot_of", [P, NT, K], U32))
            row_of = ctx.enter_context(nc.sbuf_tensor("row_of", [P, NT, K], U32))
            top_w = ctx.enter_context(nc.sbuf_tensor("top_w", [P, NT, K], F32))
            norm_phase(nc, consts, "ln0", ins["x"], xn_rows, xnT[0],
                       router=(ins["gate_wT"], table_rows, slot_of, row_of, top_w))
            qkv_phase(nc, consts, xnT[0], ins["Wqkv"], ins["bqk"], ins["bv"], qk_parts, v_rows, ffn_wT, scales)
            attention_phase(nc, consts, qk_parts, v_rows, attnT,
                            background=attention_background(nc, consts, table, slot_of, ffn_wT, scales, tern))
            experts_phase(nc, consts, xn_rows, table_rows, ins["w_gate"], ins["w_up"], ins["w_down"], y_rows)
            in_parts = [ctx.enter_context(nc.sbuf_tensor(f"in_{part}", [P, KD, 2 * DI], F32R)) for part in ("hi", "lo")]
            combine_phase(nc, consts, ins["x"], attnT, ins["Wo"], ins["bo"], y_rows, row_of, top_w, x1, xnT[1],
                          ins["in_wT"], in_parts)
            mamba_in_phase(nc, consts, xnT[1], in_parts, ins["conv_w"], ins["conv_b"], ins["x_wT"], ins["dt_wT"],
                           ins["dt_b"], xt, sg, dt, u, bc)
        scan_ffn_phase(nc, consts, xnT[1], x1, tern, scales, ins["A"], ins["Dp"], ins["out_wT"], xt, sg, dt, u, bc,
                       result)

def shape_constants():
    import numpy as np

    def bf16(a):
        return (np.ascontiguousarray(a, np.float32).view(np.uint32) >> 16).astype(np.uint16)

    row, col = np.arange(P)[:, None], np.arange(P)[None, :]
    token = np.arange(NT)[None, :] * P + np.arange(P)[:, None]
    return {
        "ident": np.eye(P, dtype=np.float32),
        "ident_b": bf16(np.eye(P)),
        "mask": bf16(np.where(col > row, -2.0 ** 127, 0)),
        "maskT": bf16(np.where(row > col, -2.0 ** 127, 0)),
        "earlier": bf16(np.triu(np.ones((P, P)), 1)),
        "iota_e": np.tile(np.arange(E, dtype=np.float32), (P, 1)),
        "tokens": token.astype(np.int32),
        "spare": (NS + token[:, :, None] * K + np.arange(K)).astype(np.float32),
    }

def kernel(**inputs):
    import numpy as np
    import concourse.bacc as bacc
    from concourse.bass_utils import run_bass_kernel_spmd

    def of(layer_part, name):
        return np.asarray(inputs[f"{layer_part}_{name}"])

    def per_partition(vector):
        return vector.reshape(-1, P).T

    bqkv = of("L0_attn", "bqkv")
    laid_out = {
        "x": of("L0_attn", "x").reshape(T, D),
        "Wqkv": of("L0_attn", "Wqkv"), "bqk": per_partition(bqkv[:2 * D]), "bv": bqkv[2 * D:],
        "Wo": of("L0_attn", "Wo"), "bo": of("L0_attn", "bo"),
        "gate_wT": of("L0_ffn", "gate_w").T,
        "w_gate": of("L0_ffn", "w_gate"), "w_up": of("L0_ffn", "w_up"), "w_down": of("L0_ffn", "w_down"),
        "in_wT": of("L1_attn", "in_proj_w").T,
        "conv_w": of("L1_attn", "conv_w"), "conv_b": per_partition(of("L1_attn", "conv_b")),
        "x_wT": of("L1_attn", "x_proj_w").T,
        "dt_wT": of("L1_attn", "dt_proj_w").T, "dt_b": per_partition(of("L1_attn", "dt_proj_b")),
        "A": of("L1_attn", "A").reshape(-1, 32, 4, 4).transpose(3, 1, 0, 2).reshape(P, -1, 4), "Dp": per_partition(of("L1_attn", "D")),
        "out_wT": of("L1_attn", "out_proj_w").T,
        "W_upT": of("L1_ffn", "W_up").T, "W_gateT": of("L1_ffn", "W_gate").T, "W_downT": of("L1_ffn", "W_down").T,
    }
    nc = bacc.Bacc("TRN2", target_bir_lowering=False, num_devices=1)
    arrays = {}

    def on_chip(group, prefix):
        handles = {}
        for name, a in group.items():
            arrays[prefix + name] = np.ascontiguousarray(a)
            handles[name] = nc.dram_tensor(prefix + name, a.shape, mybir.dt.from_np(a.dtype), kind="ExternalInput").ap()
        return handles

    ins, consts = on_chip(laid_out, "in_"), on_chip(shape_constants(), "const_")
    for name in ("ident_b", "mask", "maskT", "earlier"):
        consts[name] = consts[name].bitcast(BF16)
    result = nc.dram_tensor("out", [T, D], F32, kind="ExternalOutput").ap()
    mega_layer_kernel(nc, ins, consts, result)
    run = run_bass_kernel_spmd(nc, [arrays], core_ids=[0])
    return run.results[0]["out"].reshape(NB, L, D)
```
